# Optimizing a Trainium2 kernel written in Bass

```python
import numpy as np
import jax
import jax.numpy as jnp

def _softmax(x, axis=-1):
    return jax.nn.softmax(x, axis=axis)

def _gelu(x):
    return jax.nn.gelu(x, approximate=True)

def _silu(x):
    return jax.nn.silu(x)

def _sigmoid(x):
    return jax.nn.sigmoid(x)

def _layernorm(x, axis=-1, eps=1e-05):
    m = jnp.mean(x, axis=axis, keepdims=True)
    v = jnp.var(x, axis=axis, keepdims=True)
    return (x - m) / jnp.sqrt(v + eps)

def _scatter_add(tgt, idx, src, axis=0):
    return tgt.at[idx].add(src)

def _segment_sum(src, seg, n):
    return jax.ops.segment_sum(src, seg, n)
kernel_name = 'mk_gnn_ffn_d2_gnn_r32_c839fc'

def setup_inputs(seed: int=0):
    np.random.seed(seed)
    _w = jnp.asarray

    def _rec_inputs():
        import jax
        import jax.numpy as jnp
        _gk = jax.random.key(seed)
        x = -0.0003713 + 1 * jax.random.normal(jax.random.fold_in(_gk, 1), (3125, 256), jnp.float32)
        src = jax.random.randint(jax.random.fold_in(_gk, 2), (50000,), 0, 3125, jnp.int32)
        dst = jax.random.randint(jax.random.fold_in(_gk, 3), (50000,), 0, 3125, jnp.int32)
        _o = jnp.argsort(dst, stable=True)
        src = src[_o]
        dst = dst[_o]
        return (x, src, dst)
    x, src, dst = _rec_inputs()

    def _L0_gnn_setup():
        import jax, jax.numpy as jnp
        import numpy as np
        N_NODES = 50000
        key = jax.random.key(seed)
        k1, k2, k3 = jax.random.split(key, 3)
        x = jax.random.normal(k1, (N_NODES, 256), dtype=jnp.float32)
        edge_index = jax.random.randint(k2, (2, 50000), 0, N_NODES, dtype=jnp.int64)
        W = jax.random.normal(k3, (256, 256), dtype=jnp.float32) / np.sqrt(256.0)
        b = jnp.zeros((256,), dtype=jnp.float32)
        return {'x': x, 'edge_index': edge_index, 'W': W, 'b': b}
    _L0_gnn_all = _L0_gnn_setup()
    _L0_gnn_in = {k: v for k, v in _L0_gnn_all.items() if k in ('W', 'b')}
    del _L0_gnn_all

    def _L0_ffn_setup():
        import jax, jax.numpy as jnp
        import numpy as np
        DIM = 256
        H = 8
        D = 64
        G = 64
        INNER = H * D
        SCALE = D ** (-0.5)
        key = jax.random.key(seed)
        ks = jax.random.split(key, 12)
        B, N = (4, 512)
        x = jax.random.normal(ks[0], (B, N, DIM), dtype=jnp.float32)
        s = lambda fan_in: 1.0 / np.sqrt(fan_in)
        W_fx = jax.random.normal(ks[1], (DIM, INNER), dtype=jnp.float32) * s(DIM)
        b_fx = jnp.zeros((INNER,), dtype=jnp.float32)
        W_x = jax.random.normal(ks[2], (DIM, INNER), dtype=jnp.float32) * s(DIM)
        b_x = jnp.zeros((INNER,), dtype=jnp.float32)
        A = jax.random.normal(ks[3], (G, D), dtype=jnp.float32)
        Q, _ = jnp.linalg.qr(A.T)
        W_slice = Q[:, :G].astype(jnp.float32)
        b_slice = jnp.zeros((G,), dtype=jnp.float32)
        W_q = jax.random.normal(ks[4], (D, D), dtype=jnp.float32) * s(D)
        W_k = jax.random.normal(ks[5], (D, D), dtype=jnp.float32) * s(D)
        W_v = jax.random.normal(ks[6], (D, D), dtype=jnp.float32) * s(D)
        W_out = jax.random.normal(ks[7], (INNER, DIM), dtype=jnp.float32) * s(INNER)
        b_out = jnp.zeros((DIM,), dtype=jnp.float32)
        temperature = jnp.ones((1, H, 1, 1), dtype=jnp.float32) * 0.5
        return {'x': x, 'W_fx': W_fx, 'b_fx': b_fx, 'W_x': W_x, 'b_x': b_x, 'W_slice': W_slice, 'b_slice': b_slice, 'W_q': W_q, 'W_k': W_k, 'W_v': W_v, 'W_out': W_out, 'b_out': b_out, 'temperature': temperature}
    _L0_ffn_all = _L0_ffn_setup()
    _L0_ffn_in = {k: v for k, v in _L0_ffn_all.items() if k in ('W_fx', 'b_fx', 'W_x', 'b_x', 'W_slice', 'b_slice', 'W_q', 'W_k', 'W_v', 'W_out', 'b_out', 'temperature')}
    del _L0_ffn_all

    def _L1_gnn_setup():
        import jax, jax.numpy as jnp
        import numpy as np
        N_NODES = 3125
        F_DIM = 256
        NNZ = 50000

        def _prelu(x, a):
            return jnp.where(x >= 0, x, a * x)

        def _hconv(x, W, b, src, dst, n):
            xt = x @ W
            ones = jnp.ones(src.shape, xt.dtype)
            D = jax.ops.segment_sum(ones, src, num_segments=n)
            B = jax.ops.segment_sum(ones, dst, num_segments=n)
            Dinv = jnp.where(D > 0, 1.0 / D, 0.0)
            Binv = jnp.where(B > 0, 1.0 / B, 0.0)
            m = jax.ops.segment_sum(xt[src], dst, num_segments=n) * Binv[:, None]
            out = jax.ops.segment_sum(m[dst], src, num_segments=n) * Dinv[:, None]
            return out + b
        key = jax.random.key(seed)
        k0, k1, k2, k3 = jax.random.split(key, 4)
        x = jax.random.normal(k0, (N_NODES, F_DIM), dtype=jnp.float32)
        edge_index = jax.random.randint(k1, (2, NNZ), 0, N_NODES, dtype=jnp.int32)
        scale = (2.0 / F_DIM) ** 0.5
        W1 = jax.random.normal(k2, (F_DIM, F_DIM), dtype=jnp.float32) * scale
        W2 = jax.random.normal(k3, (F_DIM, F_DIM), dtype=jnp.float32) * scale
        b1 = jnp.zeros((F_DIM,), jnp.float32)
        b2 = jnp.zeros((F_DIM,), jnp.float32)
        a = jnp.full((1,), 0.25, jnp.float32)
        return {'x': x, 'edge_index': edge_index, 'W1': W1, 'b1': b1, 'W2': W2, 'b2': b2, 'a': a}
    _L1_gnn_all = _L1_gnn_setup()
    _L1_gnn_in = {k: v for k, v in _L1_gnn_all.items() if k in ('W1', 'b1', 'W2', 'b2', 'a')}
    del _L1_gnn_all

    def _L1_ffn_setup():
        import jax, jax.numpy as jnp
        import numpy as np
        B, T, D, H, E = (16, 128, 256, 512, 8)
        key = jax.random.key(seed)
        ks = jax.random.split(key, 5)
        x = jax.random.normal(ks[0], (B, T, D), dtype=jnp.float32)
        gate_w = jax.random.normal(ks[1], (D, E), dtype=jnp.float32) * 0.02
        gate_b = jnp.zeros((E,), dtype=jnp.float32)
        W1 = jax.random.normal(ks[2], (E, D, H), dtype=jnp.float32) * 0.02
        b1 = jnp.zeros((E, H), dtype=jnp.float32)
        W2 = jax.random.normal(ks[3], (E, H, D), dtype=jnp.float32) * 0.02
        b2 = jnp.zeros((E, D), dtype=jnp.float32)
        return {'x': x, 'gate_w': gate_w, 'gate_b': gate_b, 'W1': W1, 'b1': b1, 'W2': W2, 'b2': b2}
    _L1_ffn_all = _L1_ffn_setup()
    _L1_ffn_in = {k: v for k, v in _L1_ffn_all.items() if k in ('gate_w', 'gate_b', 'W1', 'b1', 'W2', 'b2')}
    del _L1_ffn_all
    return {'x': x, 'src': src, 'dst': dst, 'L0_gnn_W': _L0_gnn_in['W'], 'L0_gnn_b': _L0_gnn_in['b'], 'L0_ffn_W_fx': _L0_ffn_in['W_fx'], 'L0_ffn_b_fx': _L0_ffn_in['b_fx'], 'L0_ffn_W_x': _L0_ffn_in['W_x'], 'L0_ffn_b_x': _L0_ffn_in['b_x'], 'L0_ffn_W_slice': _L0_ffn_in['W_slice'], 'L0_ffn_b_slice': _L0_ffn_in['b_slice'], 'L0_ffn_W_q': _L0_ffn_in['W_q'], 'L0_ffn_W_k': _L0_ffn_in['W_k'], 'L0_ffn_W_v': _L0_ffn_in['W_v'], 'L0_ffn_W_out': _L0_ffn_in['W_out'], 'L0_ffn_b_out': _L0_ffn_in['b_out'], 'L0_ffn_temperature': _L0_ffn_in['temperature'], 'L1_gnn_W1': _L1_gnn_in['W1'], 'L1_gnn_b1': _L1_gnn_in['b1'], 'L1_gnn_W2': _L1_gnn_in['W2'], 'L1_gnn_b2': _L1_gnn_in['b2'], 'L1_gnn_a': _L1_gnn_in['a'], 'L1_ffn_gate_w': _L1_ffn_in['gate_w'], 'L1_ffn_gate_b': _L1_ffn_in['gate_b'], 'L1_ffn_W1': _L1_ffn_in['W1'], 'L1_ffn_b1': _L1_ffn_in['b1'], 'L1_ffn_W2': _L1_ffn_in['W2'], 'L1_ffn_b2': _L1_ffn_in['b2']}

def reference(x, src, dst, L0_gnn_W, L0_gnn_b, L0_ffn_W_fx, L0_ffn_b_fx, L0_ffn_W_x, L0_ffn_b_x, L0_ffn_W_slice, L0_ffn_b_slice, L0_ffn_W_q, L0_ffn_W_k, L0_ffn_W_v, L0_ffn_W_out, L0_ffn_b_out, L0_ffn_temperature, L1_gnn_W1, L1_gnn_b1, L1_gnn_W2, L1_gnn_b2, L1_gnn_a, L1_ffn_gate_w, L1_ffn_gate_b, L1_ffn_W1, L1_ffn_b1, L1_ffn_W2, L1_ffn_b2):
    import jax
    import jax.numpy as jnp

    def _L0_gnn_ref(x, edge_index, W, b):
        import jax, jax.numpy as jnp
        import numpy as np
        N_NODES = 50000
        n = x.shape[0]
        self_loops = jnp.arange(n, dtype=edge_index.dtype)
        src = jnp.concatenate([edge_index[0], self_loops])
        dst = jnp.concatenate([edge_index[1], self_loops])
        deg = jax.ops.segment_sum(jnp.ones_like(dst, dtype=x.dtype), dst, num_segments=n)
        dinv = jnp.where(deg > 0, jax.lax.rsqrt(deg), 0.0)
        norm = dinv[src] * dinv[dst]
        xw = x @ W
        msgs = xw[src] * norm[:, None]
        agg = jax.ops.segment_sum(msgs, dst, num_segments=n)
        return jax.nn.relu(agg + b)

    def _L0_ffn_ref(x, W_fx, b_fx, W_x, b_x, W_slice, b_slice, W_q, W_k, W_v, W_out, b_out, temperature):
        import jax, jax.numpy as jnp
        import numpy as np
        DIM = 256
        H = 8
        D = 64
        G = 64
        INNER = H * D
        SCALE = D ** (-0.5)
        B, N, _ = x.shape
        fx_mid = (x @ W_fx + b_fx).reshape(B, N, H, D).transpose(0, 2, 1, 3)
        x_mid = (x @ W_x + b_x).reshape(B, N, H, D).transpose(0, 2, 1, 3)
        temp = jnp.clip(temperature, 0.1, 5.0)
        slice_weights = jax.nn.softmax((x_mid @ W_slice + b_slice) / temp, axis=-1)
        slice_norm = slice_weights.sum(axis=2)
        slice_token = jnp.einsum('bhnc,bhng->bhgc', fx_mid, slice_weights)
        slice_token = slice_token / (slice_norm[..., None] + 1e-05)
        q = slice_token @ W_q
        k = slice_token @ W_k
        v = slice_token @ W_v
        attn = jax.nn.softmax(jnp.einsum('bhgc,bhkc->bhgk', q, k) * SCALE, axis=-1)
        out_slice = jnp.einsum('bhgk,bhkc->bhgc', attn, v)
        out_x = jnp.einsum('bhgc,bhng->bhnc', out_slice, slice_weights)
        out_x = out_x.transpose(0, 2, 1, 3).reshape(B, N, INNER)
        return out_x @ W_out + b_out

    def _L1_gnn_ref(x, edge_index, W1, b1, W2, b2, a):
        import jax, jax.numpy as jnp
        import numpy as np
        N_NODES = 3125
        F_DIM = 256
        NNZ = 50000

        def _prelu(x, a):
            return jnp.where(x >= 0, x, a * x)

        def _hconv(x, W, b, src, dst, n):
            xt = x @ W
            ones = jnp.ones(src.shape, xt.dtype)
            D = jax.ops.segment_sum(ones, src, num_segments=n)
            B = jax.ops.segment_sum(ones, dst, num_segments=n)
            Dinv = jnp.where(D > 0, 1.0 / D, 0.0)
            Binv = jnp.where(B > 0, 1.0 / B, 0.0)
            m = jax.ops.segment_sum(xt[src], dst, num_segments=n) * Binv[:, None]
            out = jax.ops.segment_sum(m[dst], src, num_segments=n) * Dinv[:, None]
            return out + b
        src, dst = (edge_index[0], edge_index[1])
        n = x.shape[0]
        h = _prelu(_hconv(x, W1, b1, src, dst, n), a)
        h = _hconv(h, W2, b2, src, dst, n) + x
        return _prelu(h, a)

    def _L1_ffn_ref(x, gate_w, gate_b, W1, b1, W2, b2):
        import jax, jax.numpy as jnp
        import numpy as np
        B, T, D, H, E = (16, 128, 256, 512, 8)
        Bb, Tt, Dd = x.shape
        Ee = gate_w.shape[1]
        xf = x.reshape(-1, Dd)
        N = xf.shape[0]
        logits = xf @ gate_w + gate_b
        probs = jax.nn.softmax(logits, axis=-1)
        top2_vals, top2_idx = jax.lax.top_k(probs, 2)
        cw = jnp.zeros((N, Ee), dtype=xf.dtype).at[jnp.arange(N)[:, None], top2_idx].add(top2_vals)

        def step(acc, params):
            w1, bb1, w2, bb2, we = params
            h = jax.nn.gelu(xf @ w1 + bb1, approximate=False)
            y = h @ w2 + bb2
            return (acc + we[:, None] * y, None)
        out, _ = jax.lax.scan(step, jnp.zeros_like(xf), (W1, b1, W2, b2, cw.T))
        return out.reshape(Bb, Tt, Dd)
    edge_index = jnp.stack([src, dst])
    x = x + _L0_gnn_ref(_layernorm(x, axis=-1), edge_index, L0_gnn_W, L0_gnn_b)
    x = x + _L0_ffn_ref(_layernorm(x, axis=-1)[None], L0_ffn_W_fx, L0_ffn_b_fx, L0_ffn_W_x, L0_ffn_b_x, L0_ffn_W_slice, L0_ffn_b_slice, L0_ffn_W_q, L0_ffn_W_k, L0_ffn_W_v, L0_ffn_W_out, L0_ffn_b_out, L0_ffn_temperature)[0]
    x = x + _L1_gnn_ref(_layernorm(x, axis=-1), edge_index, L1_gnn_W1, L1_gnn_b1, L1_gnn_W2, L1_gnn_b2, L1_gnn_a)
    x = x + _L1_ffn_ref(_layernorm(x, axis=-1)[None], L1_ffn_gate_w, L1_ffn_gate_b, L1_ffn_W1, L1_ffn_b1, L1_ffn_W2, L1_ffn_b2)[0]
    return x

_drawn_inputs = setup_inputs


def setup_inputs(seed=0):
    import zlib

    import numpy as np

    out = dict(_drawn_inputs(seed))
    spreads = {'L0_gnn_b': (0.0, 0.1),
     'L0_ffn_b_fx': (0.0, 0.1),
     'L0_ffn_b_x': (0.0, 0.8),
     'L0_ffn_b_slice': (0.0, 0.8),
     'L0_ffn_b_out': (0.0, 0.1),
     'L0_ffn_temperature': (0.5, 0.6),
     'L1_gnn_b1': (0.0, 0.1),
     'L1_gnn_b2': (0.0, 0.1),
     'L1_ffn_gate_b': (0.0, 0.8),
     'L1_ffn_b1': (0.0, 0.8),
     'L1_ffn_b2': (0.0, 0.541)}
    factors = {'L0_ffn_W_x': 8.0,
     'L0_ffn_W_slice': 8.0,
     'L0_ffn_W_q': 8.0,
     'L0_ffn_W_k': 8.0,
     'L1_ffn_gate_w': 3.448,
     'L1_ffn_W1': 4.968,
     'L1_ffn_W2': 4.646}
    for name, (base, spread) in spreads.items():
        noise = np.random.default_rng([zlib.crc32(name.encode()), seed]).standard_normal(out[name].shape)
        drawn = base * np.exp(spread * noise) if base else spread * noise
        out[name] = jnp.asarray(drawn.astype(out[name].dtype))
    for name, factor in factors.items():
        out[name] = (out[name] * factor).astype(out[name].dtype)
    return out
```

```python
from contextlib import ExitStack

import numpy as np
import concourse.bass as bass
from concourse import mybir

F32, F16, I32 = mybir.dt.float32, mybir.dt.float16, mybir.dt.int32
ALU, ACT, AX = mybir.AluOpType, mybir.ActivationFunctionType, mybir.AxisListType

P = 128
N, F, E = 3125, 256, 50000
NC = -(-N // P)
NP = NC * P
LAST = N - (NC - 1) * P
KF = F // P
ET = -(-E // P)
PAD_NODE = 4095
H, G, D = 8, 64, 64
INNER = H * D
NPAIR = INNER // P
X, HID = 8, 512
KH = HID // P
TILES = (2 * N + X * (P - 1)) // P
SLOTS = TILES * P
EPS = 1e-5
U = 5


class Tally:

    def __init__(self, nc, ctx, name):
        self.sem = ctx.enter_context(nc.semaphore(name))
        self.base = 0

    def at(self, k):
        return k + self.base

    def close(self, k):
        self.base += k


class Chain:

    def __init__(self, eng, tally):
        self.eng, self.tally, self.done, self.off = eng, tally, 0, 0

    def __call__(self, ins):
        self.done += 1
        ins.then_inc(self.tally.sem, 1)
        self.eng.wait_ge(self.tally.sem, self.tally.at(self.done + self.off))

    def enter(self, i, per):
        self.kept, self.per = self.done, per
        self.off = i * per

    def leave(self, trips):
        assert self.done - self.kept == self.per, (self.done - self.kept, self.per)
        self.done = self.kept + trips * self.per
        self.off = 0


def build(nc, x, src, dst, g0_w, g0_b, w_fx, b_fx, w_x, b_x, w_slice, b_slice, w_q, w_k, w_v,
          w_out, b_out, temperature, g1_w1, g1_b1, g1_w2, g1_b2, g1_a, gate_w, gate_b,
          e_w1, e_b1, e_w2, e_b2, out):
    ctx = ExitStack()
    with ctx:
        def sb(name, shape, dt=F32):
            return ctx.enter_context(nc.sbuf_tensor(name, shape, dt))

        def tally(name):
            return Tally(nc, ctx, name)

        def dram(name, shape, dt=F32):
            return nc.dram_tensor(name, shape, dt).ap()

        XR = sb("residual", [P, NC, F])
        Z = sb("normed", [P, NC, F + 4])
        SR = sb("agg_in_out", [P, 2 * NC * F])
        S = SR[:, 0:NC * F].rearrange("p (c f) -> p c f", f=F)
        R = SR[:, NC * F:2 * NC * F].rearrange("p (c f) -> p c f", f=F)
        WT = SR[:, :].rearrange("p (c k) -> p c k", k=INNER)
        BIG = sb("weights", [P, 2 * KH * X * F])
        XB = Z[:, :, :].rearrange("p c f -> p (c f)")[:, 0:X * (HID + F)]
        ident = sb("ident", [P, P])
        ones = sb("ones", [P, P])
        zeros = sb("zeros", [P, F + 4])
        before = sb("before", [P, P])
        after = sb("after", [P, P])
        iota16 = sb("iota16", [P, P], F16)
        valid = sb("valid", [P, NC])
        lane = sb("lane", [P, 1])
        ed = sb("edges_int", [P, 2, ET], I32)
        ids = sb("edge_ids", [P, 2, ET])
        deg = sb("degree", [P, 2, NC])
        inv = sb("inverse_degree", [P, 2, NC])
        dinv = sb("dinv", [P, NC])
        stats = sb("stats", [P, NC, 2])
        rstd = sb("rstd", [P, NC])
        bnbuf = sb("bnbuf", [P, NC, 6])
        gw = sb("gnn_w", [P, 3, KF, F])
        bias = sb("bias_rows", [P, 4, F])
        slope = sb("slope", [P, 1])
        tb = sb("tb", [P, 2, F])
        tT = sb("tT", [P, 2, F])
        wk = sb("wk", [P, 2, INNER])
        wn = sb("wn", [P, 2, INNER])
        sm = sb("small", [P, 2, 64])
        sm2 = sb("expert_out", [P, 2, F])
        gix = sb("gix", [P, 4], I32)
        fix = sb("fix", [P, 4])

        ps = [ctx.enter_context(nc.psum_tensor(f"bank{k}", [P, 512], F32)) for k in range(8)]

        agg_in_dram = dram("agg_in_dram", (NP, F))
        agg_out_dram = dram("agg_out_dram", (NP, F))
        xs_dram = dram("slots_in", (SLOTS, F))
        ys_dram = dram("slots_out", (SLOTS, F))

        ld, ld2, st, cst, ch, chp, cha = (tally(n) for n in (
            "loaded", "loaded2", "stored", "constants", "dve_step", "pool_step", "act_step"))
        deg_lo, deg_hi, deg_mm, y_ready = (tally(n) for n in (
            "low_onehots", "high_onehots", "degree_tile_summed", "y_ready"))
        f_idx, f_row, f_eq, f_gx, f_ga, f_mm, f_add, f_put = (tally(n) for n in (
            "edge_ids_ready", "ids_in_row", "same_target", "sources_gathered", "sums_gathered",
            "targets_summed", "sums_added", "sums_scattered"))
        t_in, t_tr, t_cp, t_mm, t_out = (tally(n) for n in (
            "row_tile_ready", "transposed", "transpose_copied", "product_ready", "product_used"))
        m_tr, m_cp, m_mm, m_out = (tally(n) for n in (
            "slices_transposed", "slices_copied", "second_product", "second_used"))
        n_a, n_b = tally("third_product"), tally("third_used")
        ysem = [tally(f"tile_stored{k}") for k in range(2)]
        gate = tally("pool_gate")
        gs = [tally(f"gathered{k}") for k in range(12)]

        primed = (deg_mm, t_in, t_tr, t_cp, t_mm, t_out, m_tr, m_cp, m_mm, m_out, n_a, n_b)
        for t in primed:
            t.close(1)
        with nc.Block() as block:
            @block.gpsimd
            def _(pool):
                for t in primed:
                    pool.sem_inc(t.sem, 1)
                step = Chain(pool, chp)
                pool.memset(ones[:], 1.0)
                pool.memset(zeros[:], 0.0)
                pool.memset(ident[:], 0.0)
                pool.memset(before[:], 1.0)
                pool.memset(after[:], 1.0)
                pool.memset(valid[:], 1.0)
                pool.memset(Z[:, :, F:F + 4], 1.0)
                pool.memset(gix[:], 0)
                pool.iota(iota16[:], [[1, P]], base=0, channel_multiplier=0,
                          allow_small_or_imprecise_dtypes=True)
                step(pool.iota(lane[:], [[0, 1]], base=0, channel_multiplier=1,
                               allow_small_or_imprecise_dtypes=True))
                pool.affine_select(out=ident[:], in_=ident[:], compare_op=ALU.not_equal, fill=1.0,
                                   base=0, pattern=[[-1, P]], channel_multiplier=1)
                pool.affine_select(out=before[:], in_=before[:], compare_op=ALU.is_gt, fill=0.0,
                                   base=0, pattern=[[1, P]], channel_multiplier=-1)
                pool.affine_select(out=after[:], in_=after[:], compare_op=ALU.is_gt, fill=0.0,
                                   base=0, pattern=[[-1, P]], channel_multiplier=1)
                pool.affine_select(out=valid[:, NC - 1:NC], in_=valid[:, NC - 1:NC],
                                   compare_op=ALU.is_gt, fill=0.0, base=LAST,
                                   pattern=[[0, 1]], channel_multiplier=-1).then_inc(cst.sem, 1)
                chp.close(step.done)

            @block.vector
            def _(dve):
                nc.vector.memset(ed[:], PAD_NODE)
                nc.vector.memset(XR[:, NC - 1, :], 0.0).then_inc(cst.sem, 1)

            @block.sync
            def _(sp):
                sp.wait_ge(cst.sem, 2)
                sp.dma_start(XR[:, 0:NC - 1, :],
                             x[0:(NC - 1) * P, :].rearrange("(c p) f -> p c f", p=P)).then_inc(ld.sem, 16)
                sp.dma_start(XR[0:LAST, NC - 1, :], x[(NC - 1) * P:N, :]).then_inc(ld.sem, 16)
                for k, e in enumerate((src, dst)):
                    full = E // ET
                    sp.dma_start(ed[0:full, k, :], e[0:full * ET].rearrange("(p j) -> p j", j=ET)
                                 ).then_inc(ld.sem, 16)
                    sp.dma_start(ed[full:full + 1, k, 0:E - full * ET],
                                 e[full * ET:E].rearrange("(p j) -> p j", p=1)).then_inc(ld.sem, 16)
                for k, w in enumerate((g0_w, g1_w1, g1_w2)):
                    sp.dma_start(gw[:, k, :, :], w.rearrange("(k p) f -> p k f", p=P)).then_inc(ld.sem, 16)
                for k, b in enumerate((g0_b, b_out, g1_b1, g1_b2)):
                    sp.dma_start(bias[:, k, :], b.partition_broadcast(P)).then_inc(ld.sem, 16)
                sp.dma_start(slope[:], g1_a.partition_broadcast(P)).then_inc(ld.sem, 16)
                sp.wait_ge(ld.sem, 16 * 14)
            ld.close(16 * 14)
            cst.close(2)

        EB = 17
        lo = SR[:, 0:2 * ET].rearrange("p (k j) -> p k j", k=2)
        hi = SR[:, 2 * ET:4 * ET].rearrange("p (k j) -> p k j", k=2)
        bits = SR[:, 4 * ET:8 * ET].bitcast(I32).rearrange("p (h k j) -> p h k j", h=2, k=2)
        oh_lo = BIG[:, 0:2 * EB * P // 2].bitcast(F16).rearrange("p (k t n) -> p k t n", k=2, n=P)
        oh_hi = BIG[:, 4096:4096 + EB * NC].bitcast(F16).rearrange("p (k t n) -> p k t n", k=2, n=NC)
        zero16 = zeros[:, 0:256].bitcast(F16)
        trips = ET // EB
        assert trips * EB == ET
        with nc.Block() as block:
            @block.vector
            def _(dve):
                step = Chain(dve, ch)
                nc.vector.tensor_single_scalar(bits[:, 0], ed[:], P - 1, ALU.bitwise_and)
                nc.vector.tensor_copy(ids[:], ed[:])
                step(nc.vector.tensor_single_scalar(bits[:, 1], ed[:], 7, ALU.logical_shift_right))
                nc.vector.tensor_copy(lo, bits[:, 0])
                step(nc.vector.tensor_copy(hi, bits[:, 1]))
                with dve.Fori(0, trips) as i:
                    dve.wait_ge(deg_mm.sem, deg_mm.at(i))
                    for k in range(2):
                        nc.vector.tensor_tensor(
                            oh_lo[:, k], iota16[:, :].unsqueeze(1).to_broadcast([P, EB, P]),
                            lo[:, k, bass.ds(i * EB, EB)].unsqueeze(2).to_broadcast([P, EB, P]),
                            ALU.is_equal).then_inc(deg_lo.sem, 1)
                        nc.vector.tensor_tensor(
                            oh_hi[:, k], iota16[:, 0:NC].unsqueeze(1).to_broadcast([P, EB, NC]),
                            hi[:, k, bass.ds(i * EB, EB)].unsqueeze(2).to_broadcast([P, EB, NC]),
                            ALU.is_equal).then_inc(deg_hi.sem, 1)
                dve.wait_ge(deg_mm.sem, deg_mm.at(trips + 1))
                for k in range(2):
                    nc.vector.tensor_copy(deg[:, k, :], ps[k][:, 0:NC])
                step(nc.vector.tensor_scalar(dinv[:], ps[1][:, 0:NC], 1.0, None, ALU.add))
                step(nc.vector.tensor_scalar(inv[:], deg[:], 1.0, None, ALU.max))
                nc.vector.reciprocal(dinv[:], dinv[:])
                step(nc.vector.reciprocal(inv[:], inv[:]))
                step(nc.vector.tensor_scalar(deg[:], deg[:], 1.0, None, ALU.min))
                nc.vector.tensor_tensor(inv[:], inv[:], deg[:], ALU.mult).then_inc(y_ready.sem, 1)
                ch.close(step.done)

            @block.tensor
            def _(pe):
                for k in range(2):
                    nc.tensor.matmul(ps[k][:, 0:NC], zero16[:, 0:P], zero16[:, 0:NC], start=True, stop=False)
                with pe.Fori(0, trips) as i:
                    pe.wait_ge(deg_lo.sem, 2 * i + 2)
                    pe.wait_ge(deg_hi.sem, 2 * i + 2)
                    for k in range(2):
                        for t in range(EB):
                            last = nc.tensor.matmul(ps[k][:, 0:NC], oh_lo[:, k, t, :], oh_hi[:, k, t, :],
                                                    start=False, stop=False)
                    last.then_inc(deg_mm.sem, 1)
                for k in range(2):
                    last = nc.tensor.matmul(ps[k][:, 0:NC], zero16[:, 0:P], zero16[:, 0:NC],
                                            start=False, stop=True)
                last.then_inc(deg_mm.sem, 1)

            @block.scalar
            def _(act):
                act.wait_ge(y_ready.sem, 1)
                nc.scalar.activation(dinv[:], dinv[:], ACT.Sqrt).then_inc(y_ready.sem, 1)

        def row(t3, c):
            return t3[:, bass.ds(c, 1), 0:F].rearrange("p a f -> p (a f)")

        def normalise():
            with nc.Block() as block:
                @block.vector
                def _(dve):
                    step = Chain(dve, ch)
                    with dve.Fori(0, NC) as c:
                        nc.vector.bn_stats(bnbuf[:, bass.ds(c, 1), :].rearrange("p a f -> p (a f)"), row(XR, c)
                                           ).then_inc(t_out.sem, 1)
                    dve.wait_ge(t_out.sem, t_out.at(NC))
                    for c in range(NC):
                        last = nc.vector.bn_aggr(stats[:, c, :], bnbuf[:, c, :])
                    step(last)
                    step(nc.vector.tensor_scalar(rstd[:], stats[:, :, 1], EPS, None, ALU.add))
                    nc.vector.reciprocal(rstd[:], rstd[:]).then_inc(t_in.sem, 1)
                    dve.wait_ge(t_cp.sem, t_cp.at(1))
                    with dve.Fori(0, NC) as c:
                        one = bass.ds(c, 1)
                        nc.vector.tensor_scalar(
                            Z[:, one, 0:F].rearrange("p a f -> p (a f)"),
                            XR[:, one, :].rearrange("p a f -> p (a f)"),
                            stats[:, one, 0:1].rearrange("p a f -> p (a f)"),
                            rstd[:, one], ALU.subtract, ALU.mult)
                    ch.close(step.done)

                @block.scalar
                def _(act):
                    act.wait_ge(t_in.sem, t_in.at(1))
                    nc.scalar.activation(rstd[:], rstd[:], ACT.Sqrt).then_inc(t_cp.sem, 1)
            t_in.close(1)
            t_cp.close(1)
            t_out.close(NC)

        def scaled_copy(dst3, src3, scale):
            with nc.Block() as block:
                @block.vector
                def _(dve):
                    step = Chain(dve, ch)
                    with dve.Fori(0, NC) as c:
                        one = bass.ds(c, 1)
                        nc.vector.tensor_scalar(
                            dst3[:, one, 0:F].rearrange("p a f -> p (a f)"),
                            src3[:, one, 0:F].rearrange("p a f -> p (a f)"),
                            scale[:, one] if scale is not None else 1.0, None, ALU.mult)
                    ch.close(step.done)

        def sum_over_edges(a, b):
            with nc.Block() as block:
                @block.sync
                def _(sp):
                    sp.dma_start(agg_in_dram.rearrange("(c p) f -> p c f", p=P), S).then_inc(st.sem, 16)
                    sp.wait_ge(st.sem, st.at(16))

                @block.gpsimd
                def _(pool):
                    for c in range(NC):
                        pool.dma_start(agg_out_dram[c * P:(c + 1) * P, :], zeros[:, 0:F]).then_inc(f_put.sem, 16)
                    pool.wait_ge(f_put.sem, f_put.at(16 * NC))
            st.close(16)
            f_put.close(16 * NC)
            with nc.Block() as block:
                @block.vector
                def _(dve):
                    step = Chain(dve, ch)
                    with dve.Fori(0, ET) as j:
                        step.enter(j, 4)
                        one = bass.ds(j, 1)
                        dve.wait_ge(f_put.sem, f_put.at(j * 16))
                        nc.vector.tensor_copy(fix[:, 0:1], ids[:, b, one])
                        nc.vector.tensor_scalar(gix[:, 0:1], ids[:, a, one], float(NP - 1), None, ALU.min)
                        nc.vector.tensor_scalar(gix[:, 1:2], ids[:, b, one], float(NP - 1), None, ALU.min)
                        step(nc.vector.tensor_copy(wk[:, 0, 0:P], ids[:, b, one].to_broadcast([P, P])))
                        dve.sem_inc(f_idx.sem, 1)
                        dve.wait_ge(f_row.sem, f_row.at(j + 1))
                        step(nc.vector.tensor_scalar(wk[:, 0, P:2 * P], ps[0][:, 0:P], fix[:, 0:1], None,
                                                     ALU.is_equal))
                        nc.vector.tensor_tensor(wn[:, 0, 0:P], wk[:, 0, P:2 * P], after[:], ALU.mult
                                                ).then_inc(f_eq.sem, 1)
                        dve.wait_ge(f_eq.sem, f_eq.at(j + 1))
                        step(nc.vector.tensor_reduce(fix[:, 1:2], wn[:, 0, 0:P], AX.X, ALU.add))
                        step(nc.vector.scalar_tensor_tensor(gix[:, 2:3], fix[:, 1:2], float(2 * PAD_NODE),
                                                            fix[:, 0:1], ALU.mult, ALU.add))
                        dve.wait_ge(f_ga.sem, f_ga.at(16 * (j + 1)))
                        dve.wait_ge(f_mm.sem, f_mm.at(j + 1))
                        nc.vector.tensor_tensor(tT[:, 0, :], tb[:, 1, :], ps[1][:, 0:F], ALU.add
                                                ).then_inc(f_add.sem, 1)
                    step.leave(ET)
                    ch.close(step.done)

                @block.tensor
                def _(pe):
                    with pe.Fori(0, ET) as j:
                        pe.wait_ge(f_idx.sem, f_idx.at(j + 1))
                        nc.tensor.matmul(ps[0][:, 0:P], wk[:, 0, 0:P], ident[:], start=True, stop=True
                                         ).then_inc(f_row.sem, 1)
                        pe.wait_ge(f_eq.sem, f_eq.at(j + 1))
                        pe.wait_ge(f_gx.sem, f_gx.at(16 * (j + 1)))
                        nc.tensor.matmul(ps[1][:, 0:F], wk[:, 0, P:2 * P], tb[:, 0, :], start=True, stop=True
                                         ).then_inc(f_mm.sem, 1)

                @block.gpsimd
                def _(pool):
                    limit = pool.to_reg(NP - 1)
                    with pool.Fori(0, ET) as j:
                        pool.wait_ge(f_idx.sem, f_idx.at(j + 1))
                        pool.sem_inc(gate.sem, 1)
                        pool.indirect_dma_start(
                            out=tb[:, 0, :], out_offset=None, in_=agg_in_dram,
                            in_offset=bass.IndirectOffsetOnAxis(ap=gix[:, 0:1], axis=0),
                            bounds_check=limit, oob_is_err=False).then_inc(f_gx.sem, 16)
                        pool.indirect_dma_start(
                            out=tb[:, 1, :], out_offset=None, in_=agg_out_dram,
                            in_offset=bass.IndirectOffsetOnAxis(ap=gix[:, 1:2], axis=0),
                            bounds_check=limit, oob_is_err=False).then_inc(f_ga.sem, 16)
                        pool.wait_ge(f_add.sem, f_add.at(j + 1))
                        pool.sem_inc(gate.sem, 1)
                        pool.indirect_dma_start(
                            out=agg_out_dram, in_=tT[:, 0, :], in_offset=None,
                            out_offset=bass.IndirectOffsetOnAxis(ap=gix[:, 2:3], axis=0),
                            bounds_check=limit, oob_is_err=False).then_inc(f_put.sem, 16)
                    pool.wait_ge(f_put.sem, f_put.at(16 * ET))
            for t, k in ((f_idx, ET), (f_row, ET), (f_eq, ET), (f_mm, ET), (f_add, ET),
                         (f_gx, 16 * ET), (f_ga, 16 * ET), (f_put, 16 * ET)):
                t.close(k)
            with nc.Block() as block:
                @block.sync
                def _(sp):
                    sp.dma_start(R, agg_out_dram.rearrange("(c p) f -> p c f", p=P)).then_inc(ld.sem, 16)
                    sp.wait_ge(ld.sem, ld.at(16))
            ld.close(16)

        def early(j):
            return -1 if j else 0

        def graph_product(kw, prepare, steps_in, consume, steps_out):
            with nc.Block() as block:
                @block.vector
                def _(dve):
                    step = Chain(dve, ch)
                    per = U * (steps_in + steps_out)
                    with dve.Fori(0, NC // U) as i:
                        step.enter(i, per)
                        for j in range(U):
                            n = i * U + j
                            dve.wait_ge(t_tr.sem, t_tr.at(n + early(j)))
                            prepare(dve, step, n, tb[:, j % 2, :])
                            dve.sem_inc(t_in.sem, 1)
                            dve.wait_ge(t_mm.sem, t_mm.at(n + 1))
                            consume(dve, step, n, ps[2 + j % 2][:, 0:F])
                            dve.sem_inc(t_out.sem, 1)
                    step.leave(NC // U)
                    ch.close(step.done)

                @block.scalar
                def _(act):
                    with act.Fori(0, NC // U) as i:
                        for j in range(U):
                            n = i * U + j
                            act.wait_ge(t_tr.sem, t_tr.at(n + 1))
                            act.wait_ge(t_mm.sem, t_mm.at(n + early(j)))
                            nc.scalar.copy(tT[:, j % 2, :], ps[j % 2][:, 0:F]).then_inc(t_cp.sem, 1)

                @block.tensor
                def _(pe):
                    with pe.Fori(0, NC // U) as i:
                        for j in range(U):
                            n = i * U + j
                            pe.wait_ge(t_in.sem, t_in.at(n + 1))
                            pe.wait_ge(t_cp.sem, t_cp.at(n + early(j)))
                            for k in range(KF):
                                last = nc.tensor.transpose(ps[j % 2][:, k * P:(k + 1) * P],
                                                           tb[:, j % 2, k * P:(k + 1) * P], ident[:])
                            last.then_inc(t_tr.sem, 1)
                            pe.wait_ge(t_cp.sem, t_cp.at(n + 1))
                            pe.wait_ge(t_out.sem, t_out.at(n + early(j)))
                            for k in range(KF):
                                last = nc.tensor.matmul(ps[2 + j % 2][:, 0:F], tT[:, j % 2, k * P:(k + 1) * P],
                                                        gw[:, kw, k, :], start=(k == 0), stop=(k == KF - 1))
                            last.then_inc(t_mm.sem, 1)
            for t in (t_in, t_tr, t_cp, t_mm, t_out):
                t.close(NC)

        normalise()
        scaled_copy(S, Z, dinv)
        sum_over_edges(0, 1)

        def take_sum(dve, step, c, dst_tile):
            step(nc.vector.tensor_tensor(dst_tile, row(R, c), row(S, c), ALU.add))

        def put_l0(dve, step, c, prod):
            step(nc.vector.scalar_tensor_tensor(wk[:, 0, 0:F], prod, dinv[:, bass.ds(c, 1)], bias[:, 0, :],
                                                ALU.mult, ALU.add))
            step(nc.vector.scalar_tensor_tensor(row(XR, c), wk[:, 0, 0:F], 0.0, row(XR, c), ALU.max, ALU.add))

        graph_product(0, take_sum, 1, put_l0, 2)
        normalise()

        wx = BIG[:, 0:KF * INNER].rearrange("p (k n) -> p k n", k=KF)
        wfx = BIG[:, 1024:1024 + KF * INNER].rearrange("p (k n) -> p k n", k=KF)
        wo = BIG[:, 2048:2048 + NPAIR * F].rearrange("p (t f) -> p t f", t=NPAIR)
        wxT = BIG[:, 3072:3072 + NPAIR * F].rearrange("p (t f) -> p t f", t=NPAIR)
        wxs = BIG[:, 4096:4096 + KF * INNER].rearrange("p (k n) -> p k n", k=KF)
        two = BIG[:, 5120:5120 + 4 * P].rearrange("p (k n) -> p k n", k=4)
        bxs = BIG[:, 5632:5632 + INNER]
        bfx = BIG[:, 6144:6144 + INNER]
        bcol = BIG[:, 6656:6656 + NPAIR]
        it = BIG[:, 6660:6660 + H]
        colb = BIG[:, 6784:6784 + INNER].rearrange("p (t m) -> p t m", t=NPAIR)
        bsl = BIG[:, 7296:7296 + G]
        with nc.Block() as block:
            @block.sync
            def _(sp):
                sp.wait_ge(cst.sem, cst.at(1))
                sp.dma_start(wx, w_x.rearrange("(k p) n -> p k n", p=P)).then_inc(ld.sem, 16)
                sp.dma_start(wfx, w_fx.rearrange("(k p) n -> p k n", p=P)).then_inc(ld.sem, 16)
                sp.dma_start(wo, w_out.rearrange("(t p) f -> p t f", p=P)).then_inc(ld.sem, 16)
                sp.dma_start(bfx, b_fx.partition_broadcast(P)).then_inc(ld.sem, 16)
                with nc.allow_non_contiguous_dma(reason="a bias as columns, once"):
                    sp.dma_start(bcol, b_x.rearrange("(t p) -> p t", p=P)).then_inc(ld.sem, 16)
                sp.dma_start(it, temperature.rearrange("a h b c -> (a h b c)").partition_broadcast(P)
                             ).then_inc(ld.sem, 16)
                sp.dma_start(bsl, b_slice.partition_broadcast(P)).then_inc(ld.sem, 16)
                for k, w in enumerate((w_slice, w_q, w_k, w_v)):
                    for h in range(2):
                        sp.dma_start(two[h * 64:h * 64 + 64, k, h * 64:h * 64 + 64], w).then_inc(ld.sem, 16)
                sp.wait_ge(ld.sem, ld.at(16 * 15))

            @block.gpsimd
            def _(pool):
                pool.memset(two, 0.0).then_inc(cst.sem, 1)
        ld.close(16 * 15)
        cst.close(1)
        with nc.Block() as block:
            @block.tensor
            def _(pe):
                for t in range(NPAIR):
                    for k in range(KF):
                        last = nc.tensor.transpose(ps[t % 2][:, (2 * (t // 2) + k) * P:(2 * (t // 2) + k + 1) * P],
                                                   wx[:, k, t * P:(t + 1) * P], ident[:])
                last.then_inc(t_tr.sem, 1)
                pe.wait_ge(t_cp.sem, t_cp.at(1))
                for k in range(KF):
                    for t in range(NPAIR):
                        nc.tensor.matmul(ps[2 + k][:, t * P:(t + 1) * P], wxT[:, t, k * P:(k + 1) * P],
                                         two[:, 0, :], start=True, stop=True)
                for t in range(NPAIR):
                    last = nc.tensor.matmul(ps[4][:, t * P:(t + 1) * P], colb[:, t, :], two[:, 0, :],
                                            start=True, stop=True)
                last.then_inc(t_mm.sem, 1)

            @block.vector
            def _(dve):
                step = Chain(dve, ch)
                step(nc.vector.tensor_scalar(it, it, 0.1, 5.0, ALU.max, ALU.min))
                step(nc.vector.reciprocal(it, it))
                nc.vector.tensor_copy(colb, bcol.unsqueeze(2).to_broadcast([P, NPAIR, P]))
                dve.wait_ge(t_tr.sem, t_tr.at(1))
                for t in range(NPAIR):
                    last = nc.vector.tensor_copy(wxT[:, t, :], ps[t % 2][:, (t // 2) * F:(t // 2) * F + F])
                last.then_inc(t_cp.sem, 1)
                dve.wait_ge(t_mm.sem, t_mm.at(1))
                it3 = it.unsqueeze(2).to_broadcast([P, H, G])
                for k in range(KF):
                    nc.vector.tensor_tensor(wxs[:, k, :].rearrange("p (h g) -> p h g", h=H),
                                            ps[2 + k][:, :].rearrange("p (h g) -> p h g", h=H), it3, ALU.mult)
                b3 = bxs.rearrange("p (h g) -> p h g", h=H)
                step(nc.vector.tensor_tensor(b3, ps[4][:, :].rearrange("p (h g) -> p h g", h=H),
                                             bsl.unsqueeze(1).to_broadcast([P, H, G]), ALU.add))
                step(nc.vector.tensor_tensor(b3, b3, it3, ALU.mult))
                ch.close(step.done)
        for t in (t_tr, t_cp, t_mm):
            t.close(1)

        def heads(t2):
            return t2.rearrange("p (h g) -> p h g", h=H)

        with nc.Block() as block:
            @block.vector
            def _(dve):
                step = Chain(dve, ch)
                per = U * 7
                with dve.Fori(0, NC // U) as i:
                    step.enter(i, per)
                    for j in range(U):
                        n, b = i * U + j, j % 2
                        dve.wait_ge(t_tr.sem, t_tr.at(n + early(j)))
                        nc.vector.tensor_copy(tb[:, b, :], row(Z, n)).then_inc(t_in.sem, 1)
                        dve.wait_ge(t_mm.sem, t_mm.at(n + 1))
                        step(nc.vector.tensor_tensor(wk[:, b, :], ps[2 + b][:, :], bxs, ALU.add))
                        dve.sem_inc(t_out.sem, 1)
                        mx, sx = sm[:, b, 0:H], sm[:, b, H:2 * H]
                        step(nc.vector.tensor_reduce(mx, heads(wk[:, b, :]), AX.X, ALU.max))
                        step(nc.vector.tensor_tensor(heads(wk[:, b, :]), heads(wk[:, b, :]),
                                                     mx.unsqueeze(2).to_broadcast([P, H, G]), ALU.subtract))
                        dve.sem_inc(m_mm.sem, 1)
                        dve.wait_ge(m_out.sem, m_out.at(n + 1))
                        step(nc.vector.tensor_reduce(sx, heads(wk[:, b, :]), AX.X, ALU.add))
                        step(nc.vector.reciprocal(sx, sx))
                        step(nc.vector.tensor_scalar(sx, sx, valid[:, bass.ds(n, 1)], None, ALU.mult))
                        dve.wait_ge(n_a.sem, n_a.at(n + early(j)))
                        step(nc.vector.tensor_tensor(heads(wn[:, b, :]), heads(wk[:, b, :]),
                                                     sx.unsqueeze(2).to_broadcast([P, H, G]), ALU.mult))
                        dve.sem_inc(n_b.sem, 1)
                step.leave(NC // U)
                ch.close(step.done)

            @block.scalar
            def _(act):
                with act.Fori(0, NC // U) as i:
                    for j in range(U):
                        n, b = i * U + j, j % 2
                        act.wait_ge(t_tr.sem, t_tr.at(n + 1))
                        act.wait_ge(t_mm.sem, t_mm.at(n + early(j)))
                        nc.scalar.copy(tT[:, b, :], ps[b][:, 0:F]).then_inc(t_cp.sem, 1)
                        act.wait_ge(m_mm.sem, m_mm.at(n + 1))
                        nc.scalar.activation(wk[:, b, :], wk[:, b, :], ACT.Exp).then_inc(m_out.sem, 1)
                        act.wait_ge(m_tr.sem, m_tr.at(n + 1))
                        nc.scalar.copy(WT[:, bass.ds(n, 1), :].rearrange("p a k -> p (a k)"), ps[b][:, :]
                                       ).then_inc(m_cp.sem, 1)

            @block.tensor
            def _(pe):
                for t in range(NPAIR):
                    nc.tensor.matmul(ps[4 + t][:, 0:F + 4], zeros[:, 0:P], zeros[:, 0:F + 4], start=True, stop=False)
                with pe.Fori(0, NC // U) as i:
                    for j in range(U):
                        n, b = i * U + j, j % 2
                        pe.wait_ge(t_in.sem, t_in.at(n + 1))
                        pe.wait_ge(m_cp.sem, m_cp.at(n + early(j)))
                        for k in range(KF):
                            last = nc.tensor.transpose(ps[b][:, k * P:(k + 1) * P], tb[:, b, k * P:(k + 1) * P],
                                                       ident[:])
                        last.then_inc(t_tr.sem, 1)
                        pe.wait_ge(t_cp.sem, t_cp.at(n + 1))
                        pe.wait_ge(t_out.sem, t_out.at(n + early(j)))
                        for k in range(KF):
                            last = nc.tensor.matmul(ps[2 + b][:, :], tT[:, b, k * P:(k + 1) * P], wxs[:, k, :],
                                                    start=(k == 0), stop=(k == KF - 1))
                        last.then_inc(t_mm.sem, 1)
                        pe.wait_ge(n_b.sem, n_b.at(n + 1))
                        for t in range(NPAIR):
                            last = nc.tensor.transpose(ps[b][:, t * P:(t + 1) * P], wn[:, b, t * P:(t + 1) * P],
                                                       ident[:])
                        last.then_inc(m_tr.sem, 1)
                        for t in range(NPAIR):
                            last = nc.tensor.matmul(ps[4 + t][:, 0:F + 4], wn[:, b, t * P:(t + 1) * P],
                                                    Z[:, bass.ds(n, 1), :].rearrange("p a f -> p (a f)"),
                                                    start=False, stop=False)
                        last.then_inc(n_a.sem, 1)
                for t in range(NPAIR):
                    last = nc.tensor.matmul(ps[4 + t][:, 0:F + 4], zeros[:, 0:P], zeros[:, 0:F + 4], start=False, stop=True)
                last.then_inc(n_a.sem, 1)
                pe.wait_ge(n_a.sem, n_a.at(NC + 1))
        for t in (t_in, t_tr, t_cp, t_mm, t_out, m_tr, m_cp, m_mm, m_out, n_b):
            t.close(NC)
        n_a.close(NC + 1)

        big0 = 7424
        xw = BIG[:, big0:big0 + NPAIR * (F + 4)].rearrange("p (t f) -> p t f", t=NPAIR)
        big1 = big0 + NPAIR * (F + 4)
        xwT = BIG[:, big1:big1 + KF * INNER].rearrange("p (k n) -> p k n", k=KF)
        big2 = big1 + KF * INNER
        tok, tokT, qT, kT, vT, att, attT = (
            BIG[:, big2 + m * INNER:big2 + (m + 1) * INNER].rearrange("p (t n) -> p t n", t=NPAIR) for m in range(7))
        big3 = big2 + 7 * INNER
        vo = BIG[:, big3:big3 + NPAIR * F].rearrange("p (t f) -> p t f", t=NPAIR)
        om = BIG[:, big3 + NPAIR * F:big3 + 2 * NPAIR * F].rearrange("p (t f) -> p t f", t=NPAIR)
        small = BIG[:, big3 + 2 * NPAIR * F:big3 + 2 * NPAIR * F + 16].rearrange("p (a t) -> p a t", t=NPAIR)
        assert big3 + 2 * NPAIR * F + 16 <= 2 * KH * X * F
        halves = [(0, slice(0, 64)), (1, slice(64, 128))]
        with nc.Block() as block:
            @block.vector
            def _(dve):
                step = Chain(dve, ch)
                for t in range(NPAIR):
                    nc.vector.tensor_copy(xw[:, t, :], ps[4 + t][:, 0:F + 4])
                nc.vector.memset(tok, 0.0)
                step(nc.vector.memset(att, 0.0))
                dve.sem_inc(t_in.sem, 1)
                dve.wait_ge(t_tr.sem, t_tr.at(1))
                for k in range(KF):
                    last = nc.vector.tensor_copy(xwT[:, k, :], ps[k][:, :])
                last.then_inc(t_cp.sem, 1)
                step(nc.vector.tensor_scalar(small[:, 0, :], xw[:, :, F], EPS, None, ALU.add))
                step(nc.vector.reciprocal(small[:, 0, :], small[:, 0, :]))
                dve.wait_ge(t_mm.sem, t_mm.at(1))
                for t in range(NPAIR):
                    for h, r in halves:
                        at = slice(t * P + 64 * h, t * P + 64 * h + 64)
                        last = nc.vector.scalar_tensor_tensor(tok[r, t, r], bfx[r, at], xw[r, t, F:F + 1],
                                                              ps[2][r, at], ALU.mult, ALU.add)
                step(last)
                for t in range(NPAIR):
                    last = nc.vector.tensor_scalar(tok[:, t, :], tok[:, t, :], small[:, 0, t:t + 1], None, ALU.mult)
                step(last)
                dve.sem_inc(t_in.sem, 1)
                dve.wait_ge(t_tr.sem, t_tr.at(2))
                nc.vector.tensor_copy(tokT, ps[0][:, :].rearrange("p (t n) -> p t n", t=NPAIR)).then_inc(t_cp.sem, 1)
                dve.wait_ge(t_mm.sem, t_mm.at(2))
                for m, to in ((1, qT), (2, kT), (3, vT)):
                    last = nc.vector.tensor_copy(to, ps[m][:, :].rearrange("p (t n) -> p t n", t=NPAIR))
                last.then_inc(t_cp.sem, 1)
                dve.wait_ge(t_mm.sem, t_mm.at(3))
                for t in range(NPAIR):
                    for h, r in halves:
                        last = nc.vector.tensor_reduce(small[r, 1, t:t + 1], ps[4][r, t * P + 64 * h:t * P + 64 * h + 64],
                                                       AX.X, ALU.max)
                step(last)
                step(nc.vector.tensor_scalar(small[:, 1, :], small[:, 1, :], -float(D) ** -0.5, None, ALU.mult))
                dve.sem_inc(m_mm.sem, 1)
                dve.wait_ge(m_out.sem, m_out.at(NPAIR * 2))
                step(nc.vector.reciprocal(small[:, 2, :], small[:, 2, :]))
                for t in range(NPAIR):
                    last = nc.vector.tensor_scalar(att[:, t, :], att[:, t, :], small[:, 2, t:t + 1], None, ALU.mult)
                step(last)
                dve.sem_inc(t_in.sem, 1)
                dve.wait_ge(t_tr.sem, t_tr.at(3))
                nc.vector.tensor_copy(attT, ps[0][:, :].rearrange("p (t n) -> p t n", t=NPAIR))
                dve.wait_ge(t_mm.sem, t_mm.at(4))
                for t in range(NPAIR):
                    last = nc.vector.tensor_copy(vo[:, t, :], ps[5 + t // 2][:, (t % 2) * F:(t % 2) * F + F])
                last.then_inc(t_cp.sem, 1)
                dve.wait_ge(t_mm.sem, t_mm.at(5))
                for t in range(NPAIR):
                    last = nc.vector.tensor_copy(om[:, t, :], ps[2 + t // 2][:, (t % 2) * F:(t % 2) * F + F])
                step(last)
                ch.close(step.done)

            @block.scalar
            def _(act):
                act.wait_ge(m_mm.sem, m_mm.at(1))
                for t in range(NPAIR):
                    for h, r in halves:
                        nc.scalar.activation(att[r, t, r], ps[4][r, t * P + 64 * h:t * P + 64 * h + 64], ACT.Exp,
                                             bias=small[r, 1, t:t + 1], scale=float(D) ** -0.5,
                                             accum_out=small[r, 2, t:t + 1]).then_inc(m_out.sem, 1)

            @block.tensor
            def _(pe):
                pe.wait_ge(t_in.sem, t_in.at(1))
                for k in range(KF):
                    for t in range(NPAIR):
                        last = nc.tensor.transpose(ps[k][:, t * P:(t + 1) * P], xw[:, t, k * P:(k + 1) * P], ident[:])
                last.then_inc(t_tr.sem, 1)
                pe.wait_ge(t_cp.sem, t_cp.at(1))
                for t in range(NPAIR):
                    for k in range(KF):
                        last = nc.tensor.matmul(ps[2][:, t * P:(t + 1) * P], xwT[:, k, t * P:(t + 1) * P],
                                                wfx[:, k, t * P:(t + 1) * P], start=(k == 0), stop=(k == KF - 1))
                last.then_inc(t_mm.sem, 1)
                pe.wait_ge(t_in.sem, t_in.at(2))
                for t in range(NPAIR):
                    last = nc.tensor.transpose(ps[0][:, t * P:(t + 1) * P], tok[:, t, :], ident[:])
                last.then_inc(t_tr.sem, 1)
                pe.wait_ge(t_cp.sem, t_cp.at(2))
                for m in (1, 2, 3):
                    last = nc.tensor.matmul(ps[m][:, :], two[:, m, :], tokT.rearrange("p t n -> p (t n)"),
                                            start=True, stop=True)
                last.then_inc(t_mm.sem, 1)
                pe.wait_ge(t_cp.sem, t_cp.at(3))
                for t in range(NPAIR):
                    last = nc.tensor.matmul(ps[4][:, t * P:(t + 1) * P], qT[:, t, :], kT[:, t, :], start=True, stop=True)
                last.then_inc(t_mm.sem, 1)
                for t in range(NPAIR):
                    last = nc.tensor.matmul(ps[5 + t // 2][:, (t % 2) * F:(t % 2) * F + F], vT[:, t, :], wo[:, t, :],
                                            start=True, stop=True)
                last.then_inc(t_mm.sem, 1)
                pe.wait_ge(t_in.sem, t_in.at(3))
                for t in range(NPAIR):
                    last = nc.tensor.transpose(ps[0][:, t * P:(t + 1) * P], att[:, t, :], ident[:])
                last.then_inc(t_tr.sem, 1)
                pe.wait_ge(t_cp.sem, t_cp.at(4))
                for t in range(NPAIR):
                    last = nc.tensor.matmul(ps[2 + t // 2][:, (t % 2) * F:(t % 2) * F + F], attT[:, t, :], vo[:, t, :],
                                            start=True, stop=True)
                last.then_inc(t_mm.sem, 1)
        for t, k in ((t_in, 3), (t_tr, 3), (t_cp, 4), (t_mm, 5), (m_mm, 1), (m_out, 2 * NPAIR)):
            t.close(k)

        with nc.Block() as block:
            @block.scalar
            def _(act):
                with act.Fori(0, NC // U) as i:
                    for j in range(U):
                        n = i * U + j
                        act.wait_ge(t_mm.sem, t_mm.at(n + early(j)))
                        nc.scalar.copy(wn[:, j % 2, :], WT[:, bass.ds(n, 1), :].rearrange("p a k -> p (a k)")
                                       ).then_inc(t_in.sem, 1)

            @block.tensor
            def _(pe):
                with pe.Fori(0, NC // U) as i:
                    for j in range(U):
                        n = i * U + j
                        pe.wait_ge(t_in.sem, t_in.at(n + 1))
                        pe.wait_ge(t_out.sem, t_out.at(n + early(j)))
                        for t in range(NPAIR):
                            last = nc.tensor.matmul(ps[j % 2][:, 0:F], wn[:, j % 2, t * P:(t + 1) * P], om[:, t, :],
                                                    start=(t == 0), stop=(t == NPAIR - 1))
                        last.then_inc(t_mm.sem, 1)

            @block.vector
            def _(dve):
                step = Chain(dve, ch)
                with dve.Fori(0, NC // U) as i:
                    step.enter(i, U * 2)
                    for j in range(U):
                        n = i * U + j
                        dve.wait_ge(t_mm.sem, t_mm.at(n + 1))
                        step(nc.vector.tensor_tensor(wk[:, j % 2, 0:F], ps[j % 2][:, 0:F], bias[:, 1, :], ALU.add))
                        dve.sem_inc(t_out.sem, 1)
                        step(nc.vector.tensor_tensor(row(XR, n), row(XR, n), wk[:, j % 2, 0:F], ALU.add))
                step.leave(NC // U)
                ch.close(step.done)
        for t in (t_in, t_mm, t_out):
            t.close(NC)

        def scale_rows(k):
            def prepare(dve, step, c, dst_tile):
                step(nc.vector.tensor_scalar(dst_tile, row(R, c), inv[:, k, bass.ds(c, 1)], None, ALU.mult))
            return prepare

        normalise()
        scaled_copy(S, Z, None)
        sum_over_edges(0, 1)
        scaled_copy(S, R, inv[:, 1, :])
        sum_over_edges(1, 0)

        def prelu(step, to, t):
            step(nc.vector.tensor_scalar(wk[:, 1, 0:F], t, 0.0, slope[:, 0:1], ALU.min, ALU.mult))
            step(nc.vector.scalar_tensor_tensor(to, t, 0.0, wk[:, 1, 0:F], ALU.max, ALU.add))

        def put_h(dve, step, c, prod):
            step(nc.vector.tensor_tensor(wk[:, 0, 0:F], prod, bias[:, 2, :], ALU.add))
            prelu(step, row(S, c), wk[:, 0, 0:F])

        graph_product(1, scale_rows(0), 1, put_h, 3)
        sum_over_edges(0, 1)
        scaled_copy(S, R, inv[:, 1, :])
        sum_over_edges(1, 0)

        def put_l1(dve, step, c, prod):
            step(nc.vector.tensor_tensor(wk[:, 0, 0:F], prod, bias[:, 3, :], ALU.add))
            step(nc.vector.tensor_tensor(wk[:, 0, 0:F], wk[:, 0, 0:F], row(Z, c), ALU.add))
            prelu(step, wk[:, 0, F:2 * F], wk[:, 0, 0:F])
            step(nc.vector.tensor_tensor(row(XR, c), row(XR, c), wk[:, 0, F:2 * F], ALU.add))

        graph_product(2, scale_rows(0), 1, put_l1, 5)
        normalise()

        w1 = BIG[:, 0:KF * X * HID].rearrange("p (k e n) -> p k e n", k=KF, e=X)
        w2 = BIG[:, KF * X * HID:2 * KF * X * HID].rearrange("p (k e n) -> p k e n", k=KH, e=X)
        b1 = XB[:, 0:X * HID].rearrange("p (e n) -> p e n", e=X)
        b2 = XB[:, X * HID:X * (HID + F)].rearrange("p (e n) -> p e n", e=X)
        gwt = gw[:, 0, :, 0:X]
        gbb = gw[:, 1, 0, 0:X]
        def table(m, w=NC * X):
            return SR[:, m * NC * X:m * NC * X + w]
        lg, prob, one1, one2, tmp, pick, rank, slot = (
            table(m).rearrange("p (c e) -> p c e", e=X) for m in range(8))
        tot = table(8)
        cum = table(9)
        mx, mx2, sx = table(10, NC), table(11, NC), table(12, NC)
        slots_f = table(13, 2 * NC).rearrange("p (k c) -> p k c", k=2)
        slots_i = table(14, 2 * NC).bitcast(I32).rearrange("p (k c) -> p k c", k=2)
        gk = table(15, 2 * NC).rearrange("p (k c) -> p k c", k=2)
        keep = table(16)
        ie = table(17, X)
        cnt = table(18, X)
        basee = table(19, X)
        tile_e = table(20, TILES)
        tile_i = table(21, TILES).bitcast(I32)
        tix = table(22, TILES)
        cmp = SR[:, 23 * NC * X:23 * NC * X + TILES * X].rearrange("p (t e) -> p t e", e=X)
        oc = SR[:, 6400:6400 + 12 * 2 * F]
        with nc.Block() as block:
            @block.sync
            def _(sp):
                for k in range(KF):
                    sp.dma_start(w1[:, k], e_w1.rearrange("e (k p) n -> k p e n", p=P)[k]).then_inc(ld.sem, 16)
                for k in range(KH):
                    sp.dma_start(w2[:, k], e_w2.rearrange("e (k p) n -> k p e n", p=P)[k]).then_inc(ld.sem, 16)
                sp.dma_start(gwt, gate_w.rearrange("(k p) e -> p k e", p=P)).then_inc(ld2.sem, 16)
                sp.dma_start(gbb, gate_b.partition_broadcast(P)).then_inc(ld2.sem, 16)
                for t in range(TILES):
                    sp.dma_start(xs_dram[t * P:(t + 1) * P, :], zeros[:, 0:F]).then_inc(st.sem, 16)
                sp.wait_ge(st.sem, st.at(16 * TILES))
                sp.wait_ge(ld.sem, ld.at(16 * (KF + KH)))
                sp.wait_ge(ld2.sem, ld2.at(32))

            @block.gpsimd
            def _(pool):
                pool.iota(ie, [[1, X]], base=0, channel_multiplier=0, allow_small_or_imprecise_dtypes=True)
                pool.iota(tix, [[P, TILES]], base=0, channel_multiplier=0, allow_small_or_imprecise_dtypes=True)
        st.close(16 * TILES)
        ld.close(16 * (KF + KH))
        ld2.close(32)
        with nc.Block() as block:
            @block.vector
            def _(dve):
                step = Chain(dve, ch)
                with dve.Fori(0, NC // U) as i:
                    step.enter(i, U)
                    for j in range(U):
                        n = i * U + j
                        dve.wait_ge(t_tr.sem, t_tr.at(n + early(j)))
                        nc.vector.tensor_copy(tb[:, j % 2, :], row(Z, n)).then_inc(t_in.sem, 1)
                        dve.wait_ge(t_mm.sem, t_mm.at(n + 1))
                        step(nc.vector.tensor_tensor(lg[:, bass.ds(n, 1), :].rearrange("p a e -> p (a e)"),
                                                     ps[2 + j % 2][:, 0:X], gbb, ALU.add))
                        dve.sem_inc(t_out.sem, 1)
                step.leave(NC // U)
                ch.close(step.done)

            @block.scalar
            def _(act):
                with act.Fori(0, NC // U) as i:
                    for j in range(U):
                        n = i * U + j
                        act.wait_ge(t_tr.sem, t_tr.at(n + 1))
                        act.wait_ge(t_mm.sem, t_mm.at(n + early(j)))
                        nc.scalar.copy(tT[:, j % 2, :], ps[j % 2][:, 0:F]).then_inc(t_cp.sem, 1)

            @block.tensor
            def _(pe):
                with pe.Fori(0, NC // U) as i:
                    for j in range(U):
                        n = i * U + j
                        pe.wait_ge(t_in.sem, t_in.at(n + 1))
                        pe.wait_ge(t_cp.sem, t_cp.at(n + early(j)))
                        for k in range(KF):
                            last = nc.tensor.transpose(ps[j % 2][:, k * P:(k + 1) * P],
                                                       tb[:, j % 2, k * P:(k + 1) * P], ident[:])
                        last.then_inc(t_tr.sem, 1)
                        pe.wait_ge(t_cp.sem, t_cp.at(n + 1))
                        pe.wait_ge(t_out.sem, t_out.at(n + early(j)))
                        for k in range(KF):
                            last = nc.tensor.matmul(ps[2 + j % 2][:, 0:X], tT[:, j % 2, k * P:(k + 1) * P],
                                                    gwt[:, k, :], start=(k == 0), stop=(k == KF - 1))
                        last.then_inc(t_mm.sem, 1)
        for t in (t_in, t_tr, t_cp, t_mm, t_out):
            t.close(NC)

        def over(t2):
            return t2.unsqueeze(2).to_broadcast([P, NC, X])

        ie3 = ie.unsqueeze(1).to_broadcast([P, NC, X])
        with nc.Block() as block:
            @block.vector
            def _(dve):
                step = Chain(dve, ch)
                step(nc.vector.tensor_reduce(mx, lg, AX.X, ALU.max))
                step(nc.vector.tensor_tensor(lg, lg, over(mx), ALU.subtract))
                dve.sem_inc(t_in.sem, 1)
                dve.wait_ge(t_cp.sem, t_cp.at(1))
                step(nc.vector.tensor_reduce(sx, prob, AX.X, ALU.add))
                step(nc.vector.reciprocal(sx, sx))
                step(nc.vector.tensor_tensor(prob, prob, over(sx), ALU.mult))
                step(nc.vector.tensor_copy(keep.rearrange("p (c e) -> p c e", e=X), prob))
                left = keep.rearrange("p (c e) -> p c e", e=X)
                for k, one in enumerate((one1, one2)):
                    top = gk[:, k, :]
                    step(nc.vector.tensor_reduce(top, left, AX.X, ALU.max))
                    step(nc.vector.tensor_tensor(tmp, left, over(top), ALU.is_lt))
                    step(nc.vector.scalar_tensor_tensor(tmp, tmp, float(X), ie3, ALU.mult, ALU.add))
                    step(nc.vector.tensor_reduce(mx2, tmp, AX.X, ALU.min))
                    step(nc.vector.tensor_tensor(one, ie3, over(mx2), ALU.is_equal))
                    step(nc.vector.scalar_tensor_tensor(left, one, -2.0, left, ALU.mult, ALU.add))
                step(nc.vector.tensor_tensor(pick, one1, one2, ALU.add))
                step(nc.vector.tensor_tensor(pick, pick, over(valid[:]), ALU.mult))
                dve.sem_inc(t_in.sem, 1)
                dve.wait_ge(t_mm.sem, t_mm.at(1))
                nc.vector.tensor_copy(rank.rearrange("p c e -> p (c e)"), ps[0][:, 0:NC * X])
                step(nc.vector.tensor_copy(tot.rearrange("p (e c) -> p e c", e=X),
                                           ps[1][:, 0:NC * X].rearrange("p (c e) -> p e c", e=X)))
                for e in range(X):
                    at = slice(e * NC, (e + 1) * NC)
                    last = nc.vector.tensor_tensor_scan(cum[:, at], tot[:, at], tot[:, at], 0.0, ALU.add, ALU.bypass)
                step(last)
                step(nc.vector.tensor_copy(cnt, cum.rearrange("p (e c) -> p e c", e=X)[:, :, NC - 1]))
                step(nc.vector.tensor_tensor(cum, cum, tot, ALU.subtract))
                step(nc.vector.tensor_tensor(cmp, tix.unsqueeze(2).to_broadcast([P, TILES, X]),
                                             cnt.unsqueeze(1).to_broadcast([P, TILES, X]), ALU.is_lt))
                step(nc.vector.tensor_reduce(cnt, cmp.rearrange("p t e -> p e t"), AX.X, ALU.add))
                step(nc.vector.tensor_tensor_scan(basee, cnt, cnt, 0.0, ALU.add, ALU.bypass))
                step(nc.vector.tensor_scalar(tmp[:, 0, :], basee, float(P), None, ALU.mult))
                step(nc.vector.tensor_tensor(cmp, tix.unsqueeze(2).to_broadcast([P, TILES, X]),
                                             tmp[:, 0, :].unsqueeze(1).to_broadcast([P, TILES, X]), ALU.is_ge))
                step(nc.vector.tensor_reduce(tile_e, cmp, AX.X, ALU.add))
                step(nc.vector.tensor_scalar(tile_e, tile_e, float(X - 1), None, ALU.min))
                step(nc.vector.tensor_copy(tile_i, tile_e))
                step(nc.vector.tensor_tensor(basee, basee, cnt, ALU.subtract))
                step(nc.vector.tensor_scalar(basee, basee, float(P), None, ALU.mult))
                step(nc.vector.tensor_tensor(slot, rank, cum.rearrange("p (e c) -> p c e", e=X), ALU.add))
                step(nc.vector.tensor_tensor(slot, slot, basee.unsqueeze(1).to_broadcast([P, NC, X]), ALU.add))
                for k, one in enumerate((one1, one2)):
                    step(nc.vector.tensor_tensor(tmp, slot, one, ALU.mult))
                    step(nc.vector.tensor_reduce(slots_f[:, k, :], tmp, AX.X, ALU.add))
                step(nc.vector.tensor_scalar(mx, valid[:], -float(4 * SLOTS), float(4 * SLOTS), ALU.mult, ALU.add))
                for k in range(2):
                    step(nc.vector.tensor_tensor(slots_f[:, k, :], slots_f[:, k, :], mx, ALU.add))
                step(nc.vector.tensor_copy(slots_i, slots_f))
                ch.close(step.done)

            @block.scalar
            def _(act):
                act.wait_ge(t_in.sem, t_in.at(1))
                nc.scalar.activation(prob, lg, ACT.Exp).then_inc(t_cp.sem, 1)

            @block.tensor
            def _(pe):
                pe.wait_ge(t_in.sem, t_in.at(2))
                nc.tensor.matmul(ps[0][:, 0:NC * X], before[:], pick.rearrange("p c e -> p (c e)"), start=True, stop=True)
                nc.tensor.matmul(ps[1][:, 0:NC * X], ones[:], pick.rearrange("p c e -> p (c e)"), start=True, stop=True
                                 ).then_inc(t_mm.sem, 1)
        for t, k in ((t_in, 2), (t_cp, 1), (t_mm, 1)):
            t.close(k)

        with nc.Block() as block:
            @block.gpsimd
            def _(pool):
                for c in range(NC):
                    for k in range(2):
                        pool.indirect_dma_start(
                            out=xs_dram, in_=Z[:, c, 0:F], in_offset=None,
                            out_offset=bass.IndirectOffsetOnAxis(ap=slots_i[:, k, c:c + 1], axis=0),
                            bounds_check=SLOTS - 1, oob_is_err=False).then_inc(ysem[k].sem, 16)
                for k in range(2):
                    pool.wait_ge(ysem[k].sem, ysem[k].at(16 * NC))
        for t in ysem:
            t.close(16 * NC)
        with nc.Block() as block:
            @block.sync
            def _(sp):
                sp.dma_start(b1.rearrange("p e n -> p (e n)"), e_b1.rearrange("e n -> (e n)").partition_broadcast(P)).then_inc(ld.sem, 16)
                sp.dma_start(b2.rearrange("p e n -> p (e n)"), e_b2.rearrange("e n -> (e n)").partition_broadcast(P)).then_inc(ld.sem, 16)
                sp.wait_ge(ld.sem, ld.at(32))
        ld.close(32)

        UT = 2
        assert TILES % UT == 0
        hT = wk
        with nc.Block() as block:
            @block.sync
            def _(sp):
                with sp.Fori(0, TILES // UT) as i:
                    for j in range(UT):
                        n = i * UT + j
                        if j == 0:
                            sp.wait_ge(t_tr.sem, t_tr.at(n))
                        else:
                            sp.wait_ge(t_tr.sem, t_tr.at(n - 1))
                        sp.dma_start(tb[:, j, :], xs_dram[bass.ds(n * P, P), :]).then_inc((ld, ld2)[j].sem, 16)

            @block.tensor
            def _(pe):
                with pe.Fori(0, TILES // UT) as i:
                    for j in range(UT):
                        n = i * UT + j
                        pe.wait_ge((ld, ld2)[j].sem, (ld, ld2)[j].at(16 * i + 16))
                        pe.wait_ge(m_cp.sem, m_cp.at(n - j))
                        expert = pe.value_load(tile_i[0:1, bass.ds(n, 1)], min_val=0, max_val=X - 1)
                        for k in range(KF):
                            last = nc.tensor.transpose(ps[j][:, k * P:(k + 1) * P], tb[:, j, k * P:(k + 1) * P], ident[:])
                        last.then_inc(t_tr.sem, 1)
                        pe.wait_ge(t_cp.sem, t_cp.at(n + 1))
                        pe.wait_ge(t_out.sem, t_out.at(n - j))
                        for k in range(KF):
                            last = nc.tensor.matmul(ps[2 + j][:, :], tT[:, j, k * P:(k + 1) * P],
                                                    w1[:, k, bass.ds(expert, 1), :].rearrange("p a n -> p (a n)"),
                                                    start=(k == 0), stop=(k == KF - 1))
                        last.then_inc(t_mm.sem, 1)
                        pe.wait_ge(m_mm.sem, m_mm.at(n + 1))
                        for k in range(KH):
                            last = nc.tensor.transpose(ps[j][:, k * P:(k + 1) * P], wn[:, j, k * P:(k + 1) * P], ident[:])
                        last.then_inc(m_tr.sem, 1)
                        pe.wait_ge(m_cp.sem, m_cp.at(n + 1))
                        pe.wait_ge(n_b.sem, n_b.at(n - j))
                        for k in range(KH):
                            last = nc.tensor.matmul(ps[4 + j][:, 0:F], hT[:, j, k * P:(k + 1) * P],
                                                    w2[:, k, bass.ds(expert, 1), :].rearrange("p a n -> p (a n)"),
                                                    start=(k == 0), stop=(k == KH - 1))
                        last.then_inc(n_a.sem, 1)

            @block.vector
            def _(dve):
                with dve.Fori(0, TILES // UT) as i:
                    for j in range(UT):
                        n = i * UT + j
                        expert = dve.value_load(tile_i[0:1, bass.ds(n, 1)], min_val=0, max_val=X - 1)
                        dve.wait_ge(t_mm.sem, t_mm.at(n + 1))
                        dve.wait_ge(m_tr.sem, m_tr.at(n - j))
                        nc.vector.tensor_tensor(wn[:, j, :], ps[2 + j][:, :],
                                                b1[:, bass.ds(expert, 1), :].rearrange("p a n -> p (a n)"), ALU.add
                                                ).then_inc(t_out.sem, 1)
                        dve.wait_ge(m_tr.sem, m_tr.at(n + 1))
                        dve.wait_ge(n_a.sem, n_a.at(n - j))
                        nc.vector.tensor_copy(hT[:, j, :], ps[j][:, :]).then_inc(m_cp.sem, 1)
                        dve.wait_ge(n_a.sem, n_a.at(n + 1))
                        dve.wait_ge(ysem[j].sem, ysem[j].at(16 * i))
                        nc.vector.tensor_tensor(sm2[:, j, :], ps[4 + j][:, 0:F],
                                                b2[:, bass.ds(expert, 1), :].rearrange("p a n -> p (a n)"), ALU.add
                                                ).then_inc(n_b.sem, 1)

            @block.scalar
            def _(act):
                with act.Fori(0, TILES // UT) as i:
                    for j in range(UT):
                        n = i * UT + j
                        act.wait_ge(t_tr.sem, t_tr.at(n + 1))
                        act.wait_ge(t_mm.sem, t_mm.at(n - j))
                        nc.scalar.copy(tT[:, j, :], ps[j][:, 0:F]).then_inc(t_cp.sem, 1)
                        act.wait_ge(t_out.sem, t_out.at(n + 1))
                        nc.scalar.activation(wn[:, j, :], wn[:, j, :], ACT.Gelu).then_inc(m_mm.sem, 1)

            @block.gpsimd
            def _(pool):
                with pool.Fori(0, TILES // UT) as i:
                    for j in range(UT):
                        n = i * UT + j
                        pool.wait_ge(n_b.sem, n_b.at(n + 1))
                        pool.dma_start(ys_dram[bass.ds(n * P, P), :], sm2[:, j, :]).then_inc(ysem[j].sem, 16)
                for j in range(UT):
                    pool.wait_ge(ysem[j].sem, ysem[j].at(16 * (TILES // UT)))
        for t in (t_tr, t_cp, t_mm, t_out, m_mm, m_tr, m_cp, n_a, n_b):
            t.close(TILES)
        for t in (*ysem, ld, ld2):
            t.close(16 * (TILES // UT))

        oc4 = oc.rearrange("p (b k f) -> p b k f", k=2, f=F)
        NB = 12
        with nc.Block() as block:
            @block.gpsimd
            def _(pool):
                pool.memset(oc, 0.0).then_inc(chp.sem, 1)
                pool.wait_ge(chp.sem, chp.at(1))
                for c in range(NC):
                    if c >= NB:
                        pool.wait_ge(t_out.sem, t_out.at(c - NB + 1))
                    for k in range(2):
                        pool.indirect_dma_start(
                            out=oc4[:, c % NB, k, :], out_offset=None, in_=ys_dram,
                            in_offset=bass.IndirectOffsetOnAxis(ap=slots_i[:, k, c:c + 1], axis=0),
                            bounds_check=SLOTS - 1, oob_is_err=False).then_inc(gs[c % NB].sem, 16)

            @block.vector
            def _(dve):
                step = Chain(dve, ch)
                for c in range(NC):
                    dve.wait_ge(gs[c % NB].sem, 32 * (c // NB + 1))
                    step(nc.vector.scalar_tensor_tensor(XR[:, c, :], oc4[:, c % NB, 0, :], gk[:, 0, c:c + 1],
                                                        XR[:, c, :], ALU.mult, ALU.add))
                    step(nc.vector.scalar_tensor_tensor(XR[:, c, :], oc4[:, c % NB, 1, :], gk[:, 1, c:c + 1],
                                                        XR[:, c, :], ALU.mult, ALU.add))
                    dve.sem_inc(t_out.sem, 1)
                ch.close(step.done)

            @block.sync
            def _(sp):
                sp.wait_ge(t_out.sem, t_out.at(NC))
                sp.dma_start(out[0:(NC - 1) * P, :].rearrange("(c p) f -> p c f", p=P), XR[:, 0:NC - 1, :]).then_inc(st.sem, 16)
                sp.dma_start(out[(NC - 1) * P:N, :], XR[0:LAST, NC - 1, :]).then_inc(st.sem, 16)
                sp.wait_ge(st.sem, st.at(32))


_INS = ['x', 'src', 'dst', 'L0_gnn_W', 'L0_gnn_b', 'L0_ffn_W_fx', 'L0_ffn_b_fx', 'L0_ffn_W_x', 'L0_ffn_b_x',
        'L0_ffn_W_slice', 'L0_ffn_b_slice', 'L0_ffn_W_q', 'L0_ffn_W_k', 'L0_ffn_W_v', 'L0_ffn_W_out',
        'L0_ffn_b_out', 'L0_ffn_temperature', 'L1_gnn_W1', 'L1_gnn_b1', 'L1_gnn_W2', 'L1_gnn_b2', 'L1_gnn_a',
        'L1_ffn_gate_w', 'L1_ffn_gate_b', 'L1_ffn_W1', 'L1_ffn_b1', 'L1_ffn_W2', 'L1_ffn_b2']


def kernel(**inputs):
    import concourse.bacc as bacc
    from concourse.bass_utils import run_bass_kernel_spmd

    nc = bacc.Bacc("TRN2", target_bir_lowering=False, num_devices=1)
    arrays, args = {}, []
    for name in _INS:
        a = np.ascontiguousarray(inputs[name])
        arrays[f"in_{name}"] = a
        args.append(nc.dram_tensor(f"in_{name}", a.shape, mybir.dt.from_np(a.dtype), kind="ExternalInput").ap())
    args.append(nc.dram_tensor("out_0", (N, F), F32, kind="ExternalOutput").ap())
    build(nc, *args)
    r = run_bass_kernel_spmd(nc, [arrays], core_ids=[0])
    return r.results[0]["out_0"]
```

```python
from contextlib import ExitStack

import numpy as np
import concourse.bass as bass
from concourse import mybir

F32, F16, I32 = mybir.dt.float32, mybir.dt.float16, mybir.dt.int32
ALU, ACT, AX = mybir.AluOpType, mybir.ActivationFunctionType, mybir.AxisListType

P = 128
N, F, E = 3125, 256, 50000
NC = -(-N // P)
NP = NC * P
LAST = N - (NC - 1) * P
KF = F // P
EW = 400
ER = E // EW
ET = EW
GN = 5
SB = 5 * P
NSB = NP // SB
GROUPS = NP // GN
STEP = 8
WROWS = E // STEP + STEP
FIX = 1024.0
BIGH = 8192.0
PAD_NODE = 4095
H, G, D = 8, 64, 64
INNER = H * D
NPAIR = INNER // P
X, HID = 8, 512
KH = HID // P
TILES = (2 * N + X * (P - 1)) // P
SLOTS = TILES * P
EPS = 1e-5
U = 5


class Tally:

    def __init__(self, nc, ctx, name):
        self.sem = ctx.enter_context(nc.semaphore(name))
        self.base = 0

    def at(self, k):
        return k + self.base

    def close(self, k):
        self.base += k


class Chain:

    def __init__(self, eng, tally):
        self.eng, self.tally, self.done, self.off = eng, tally, 0, 0

    def __call__(self, ins):
        self.done += 1
        ins.then_inc(self.tally.sem, 1)
        self.eng.wait_ge(self.tally.sem, self.tally.at(self.done + self.off))

    def enter(self, i, per):
        self.kept, self.per = self.done, per
        self.off = i * per

    def leave(self, trips):
        assert self.done - self.kept == self.per, (self.done - self.kept, self.per)
        self.done = self.kept + trips * self.per
        self.off = 0


def build(nc, x, src, dst, g0_w, g0_b, w_fx, b_fx, w_x, b_x, w_slice, b_slice, w_q, w_k, w_v,
          w_out, b_out, temperature, g1_w1, g1_b1, g1_w2, g1_b2, g1_a, gate_w, gate_b,
          e_w1, e_b1, e_w2, e_b2, out):
    ctx = ExitStack()
    with ctx:
        def sb(name, shape, dt=F32):
            return ctx.enter_context(nc.sbuf_tensor(name, shape, dt))

        def tally(name):
            return Tally(nc, ctx, name)

        def dram(name, shape, dt=F32):
            return nc.dram_tensor(name, shape, dt).ap()

        XR = sb("residual", [P, NC, F])
        Z = sb("normed", [P, NC, F + 4])
        SR = sb("agg_in_out", [P, 2 * NC * F])
        S = SR[:, 0:NC * F].rearrange("p (c f) -> p c f", f=F)
        R = SR[:, NC * F:2 * NC * F].rearrange("p (c f) -> p c f", f=F)
        WT = SR[:, :].rearrange("p (c k) -> p c k", k=INNER)
        BIG = sb("weights", [P, 2 * KH * X * F])
        XB = Z[:, :, :].rearrange("p c f -> p (c f)")[:, 0:X * (HID + F)]
        ident = sb("ident", [P, P])
        ones = sb("ones", [P, P])
        zeros = sb("zeros", [P, F + 4])
        before = sb("before", [P, P])
        after = sb("after", [P, P])
        iota16 = sb("iota16", [P, P], F16)
        valid = sb("valid", [P, NC])
        lane = sb("lane", [P, 1])
        flag = sb("flag", [P, 1], I32)
        ids = sb("edge_ids", [P, 2, ET])
        deg = sb("degree", [P, 2, NC + 1])
        inv = sb("inverse_degree", [P, 2, NC])
        invs = sb("unscaling", [P, 2, NC])
        hmax = sb("largest", [P, NC + 3])
        dinv = sb("dinv", [P, NC])
        dinvs = sb("dinv_unscaled", [P, NC])
        stats = sb("stats", [P, NC, 2])
        rstd = sb("rstd", [P, NC])
        bnbuf = sb("bnbuf", [P, NC, 6])
        gw = sb("gnn_w", [P, 3, KF, F])
        bias = sb("bias_rows", [P, 4, F])
        slope = sb("slope", [P, 1])
        tb = sb("tb", [P, 2, F])
        tT = sb("tT", [P, 2, F])
        wk = sb("wk", [P, 2, INNER])
        wn = sb("wn", [P, 2, INNER])
        sm = sb("small", [P, 2, 64])
        padkeys = sb("padding_keys", [1, 2 * P])
        ident16 = sb("ident16", [P, P], F16)
        sm2 = sb("expert_out", [P, 2, F])
        gix = sb("gix", [P, 4], I32)
        fix = sb("fix", [P, 4])

        ps = [ctx.enter_context(nc.psum_tensor(f"bank{k}", [P, 512], F32)) for k in range(8)]

        packed_dram = dram("edges_packed", (WROWS * STEP + P,))
        window_dram = dram("edge_windows", (WROWS, P))
        below_dram = dram("edges_below", ((NC + 1) * P,), I32)
        at_dram = dram("counts_source_target", (NP, NP), F16)
        a_dram = dram("counts_target_source", (NP, NP), F16)
        agg_in_dram = dram("agg_in_dram", (NP, F))
        agg_out_dram = dram("agg_out_dram", (NP, F))
        xs_dram = dram("slots_in", (SLOTS, F))
        ys_dram = dram("slots_out", (SLOTS, F))

        ld, ld2, st, cst, ch, chp, cha = (tally(n) for n in (
            "loaded", "loaded2", "stored", "constants", "dve_step", "pool_step", "act_step"))
        deg_lo, deg_hi, deg_mm, y_ready = (tally(n) for n in (
            "low_onehots", "high_onehots", "degree_tile_summed", "y_ready"))
        f_idx, f_row, f_eq, f_gx, f_ga, f_mm, f_add, f_put = (tally(n) for n in (
            "edge_ids_ready", "ids_in_row", "same_target", "sources_gathered", "sums_gathered",
            "targets_summed", "sums_added", "sums_scattered"))
        t_in, t_tr, t_cp, t_mm, t_out = (tally(n) for n in (
            "row_tile_ready", "transposed", "transpose_copied", "product_ready", "product_used"))
        m_tr, m_cp, m_mm, m_out = (tally(n) for n in (
            "slices_transposed", "slices_copied", "second_product", "second_used"))
        n_a, n_b = tally("third_product"), tally("third_used")
        ysem = [tally(f"tile_stored{k}") for k in range(2)]
        st2 = tally("windows_stored")
        q_in, q_mm, q_ev, r_tr, r_act, r_dve = (tally(n) for n in (
            "quad_onehots", "quad_counted", "quad_copied", "row_transposed", "row_copied_act", "row_copied_dve"))
        s_st = [tally(f"superblock_stored{k}") for k in range(2)]
        r_st = [tally(f"row_stored{k}") for k in range(5)]
        f_src, f_st, f_ld, chg = (tally(n) for n in (
            "rows_made", "rows_stored", "sums_loaded", "general_dve_step"))
        a_in, a_mm, a_lo, a_ev, a_kb = (tally(n) for n in (
            "halves_ready", "sums_ready", "low_sum_copied", "sums_out", "matrix_rows_used"))
        a_ld = [tally(f"matrix_rows_loaded{k}") for k in range(5)]
        gate, s_gate = tally("pool_gate"), tally("sp_gate")
        gs = [tally(f"gathered{k}") for k in range(12)]

        def space(at, w):
            return SR[:, at:at + w]
        ed = space(0, 2 * ET).bitcast(I32).rearrange("p (k j) -> p k j", k=2)
        bits = space(800, 4 * ET).bitcast(I32).rearrange("p (h k j) -> p h k j", h=2, k=2)
        lo = space(2400, 2 * ET).rearrange("p (k j) -> p k j", k=2)
        hi = space(3200, 2 * ET).rearrange("p (k j) -> p k j", k=2)
        key = space(4000, EW)
        worse = space(4400, EW)
        bad = space(4800, 8)
        nxt = space(4808, 1).bitcast(I32)
        below = space(4810, NC + 1)
        run = space(4840, 2 * (NC + 1)).rearrange("p (a c) -> p a c", a=2)
        belowT = space(4900, P).bitcast(I32)
        starts = space(5030, 2 * NSB).bitcast(I32).rearrange("p (k b) -> p k b", k=2)
        first = space(5040, NSB).bitcast(I32)
        startf = space(5046, 2 * NSB).rearrange("p (k b) -> p k b", k=2)
        gbase = space(5060, GROUPS)
        win = space(6400, NSB * P).rearrange("p (b e) -> p b e", b=NSB)
        wbits = space(7040, 4 * GROUPS).bitcast(I32).rearrange("p (h g) -> p h g", h=4)
        wf = space(9600, 3 * GROUPS).rearrange("p (h g) -> p h g", h=3)
        rk, slo = (sb(n, [P, GROUPS]) for n in ("row_of_edge", "low_source"))

        primed = [(t, 1) for t in (deg_mm, t_in, t_tr, t_cp, t_mm, t_out, m_tr, m_cp, m_mm, m_out, n_a, n_b,
                                   r_act, r_dve)]
        primed += [(q_mm, 4), (q_ev, 4), (r_tr, 26), (a_ev, 6), (a_kb, 6), (a_mm, 1)]
        for t, k in primed:
            t.close(k)
        with nc.Block() as block:
            @block.gpsimd
            def _(pool):
                for t, k in primed:
                    pool.sem_inc(t.sem, k)
                step = Chain(pool, chp)
                pool.memset(ones[:], 1.0)
                pool.memset(zeros[:], 0.0)
                pool.memset(ident[:], 0.0)
                pool.memset(before[:], 1.0)
                pool.memset(after[:], 1.0)
                pool.memset(valid[:], 1.0)
                pool.memset(Z[:, :, F:F + 4], 1.0)
                pool.memset(gix[:], 0)
                pool.memset(padkeys[:], float((PAD_NODE + 1) ** 2 - 1))
                pool.iota(gbase, [[GN, GROUPS]], base=0, channel_multiplier=0,
                          allow_small_or_imprecise_dtypes=True)
                pool.iota(iota16[:], [[1, P]], base=0, channel_multiplier=0,
                          allow_small_or_imprecise_dtypes=True)
                step(pool.iota(lane[:], [[0, 1]], base=0, channel_multiplier=1,
                               allow_small_or_imprecise_dtypes=True))
                step(pool.affine_select(out=ident[:], in_=ident[:], compare_op=ALU.not_equal, fill=1.0,
                                        base=0, pattern=[[-1, P]], channel_multiplier=1))
                pool.affine_select(out=before[:], in_=before[:], compare_op=ALU.is_gt, fill=0.0,
                                   base=0, pattern=[[1, P]], channel_multiplier=-1)
                pool.affine_select(out=after[:], in_=after[:], compare_op=ALU.is_gt, fill=0.0,
                                   base=0, pattern=[[-1, P]], channel_multiplier=1)
                pool.affine_select(out=valid[:, NC - 1:NC], in_=valid[:, NC - 1:NC],
                                   compare_op=ALU.is_gt, fill=0.0, base=LAST,
                                   pattern=[[0, 1]], channel_multiplier=-1).then_inc(cst.sem, 1)
                pool.tensor_copy(ident16[:], ident[:])
                chp.close(step.done)

            @block.vector
            def _(dve):
                nc.vector.memset(ed, PAD_NODE)
                nc.vector.memset(nxt, PAD_NODE)
                nc.vector.memset(XR[:, NC - 1, :], 0.0).then_inc(cst.sem, 1)

            @block.sync
            def _(sp):
                sp.wait_ge(cst.sem, 2)
                sp.dma_start(XR[:, 0:NC - 1, :],
                             x[0:(NC - 1) * P, :].rearrange("(c p) f -> p c f", p=P)).then_inc(ld.sem, 16)
                sp.dma_start(XR[0:LAST, NC - 1, :], x[(NC - 1) * P:N, :]).then_inc(ld.sem, 16)
                for k, e in enumerate((src, dst)):
                    sp.dma_start(ed[0:ER, k, :], e.rearrange("(p j) -> p j", j=EW)).then_inc(ld.sem, 16)
                with nc.allow_non_contiguous_dma(reason="one number per partition, once"):
                    sp.dma_start(nxt[0:ER - 1, :], dst[EW:E].rearrange("(p j) -> p j", j=EW)[:, 0:1]
                                 ).then_inc(ld.sem, 16)
                for k, w in enumerate((g0_w, g1_w1, g1_w2)):
                    sp.dma_start(gw[:, k, :, :], w.rearrange("(k p) f -> p k f", p=P)).then_inc(r_st[k].sem, 16)
                for k, b in enumerate((g0_b, b_out, g1_b1, g1_b2)):
                    sp.dma_start(bias[:, k, :], b.partition_broadcast(P)).then_inc((*r_st, *s_st)[3 + k].sem, 16)
                sp.dma_start(slope[:], g1_a.partition_broadcast(P)).then_inc(ld.sem, 16)
                sp.wait_ge(ld.sem, 16 * 6)
                for t in (*r_st, *s_st):
                    sp.wait_ge(t.sem, 16)
            ld.close(16 * 6)
            for t in (*r_st, *s_st):
                t.close(16)
            cst.close(2)

        EB = 16
        oh_lo = BIG[:, 0:2 * EB * P // 2].bitcast(F16).rearrange("p (k t n) -> p k t n", k=2, n=P)
        oh_hi = BIG[:, 4096:4096 + EB * NC].bitcast(F16).rearrange("p (k t n) -> p k t n", k=2, n=NC)
        zero16 = zeros[:, 0:256].bitcast(F16)
        trips = ET // EB
        assert trips * EB == ET
        with nc.Block() as block:
            @block.vector
            def _(dve):
                step = Chain(dve, ch)
                nc.vector.tensor_single_scalar(bits[:, 0], ed, P - 1, ALU.bitwise_and)
                nc.vector.tensor_copy(ids[:], ed)
                step(nc.vector.tensor_single_scalar(bits[:, 1], ed, 7, ALU.logical_shift_right))
                nc.vector.tensor_copy(lo, bits[:, 0])
                step(nc.vector.tensor_copy(hi, bits[:, 1]))
                nc.vector.scalar_tensor_tensor(key, ids[:, 1], float(PAD_NODE + 1), ids[:, 0], ALU.mult, ALU.add
                                               ).then_inc(y_ready.sem, 1)
                nc.vector.tensor_tensor(worse[:, 0:EW - 1], ids[:, 1, 1:EW], ids[:, 1, 0:EW - 1], ALU.is_lt)
                nc.vector.tensor_copy(bad[:, 1:2], nxt)
                step(nc.vector.memset(deg[:], 0.0))
                nc.vector.tensor_tensor(worse[:, EW - 1:EW], bad[:, 1:2], ids[:, 1, EW - 1:EW], ALU.is_lt)
                step(nc.vector.memset(bad[:, 4:5], 0.0))
                step(nc.vector.tensor_reduce(bad[:, 0:1], worse, AX.X, ALU.max))
                with dve.Fori(0, trips) as i:
                    dve.wait_ge(deg_mm.sem, deg_mm.at(i))
                    for k in range(2):
                        nc.vector.tensor_tensor(
                            oh_hi[:, k], iota16[:, 0:NC].unsqueeze(1).to_broadcast([P, EB, NC]),
                            hi[:, k, bass.ds(i * EB, EB)].unsqueeze(2).to_broadcast([P, EB, NC]), ALU.is_equal)
                        for t in range(EB):
                            last = nc.vector.tensor_scalar(oh_lo[:, k, t, :], iota16[:, :],
                                                           lo[:, k, bass.ds(i * EB + t, 1)], None, ALU.is_equal)
                    last.then_inc(deg_lo.sem, 1)
                dve.wait_ge(deg_mm.sem, deg_mm.at(trips + 1))
                step(nc.vector.tensor_scalar(dinv[:], ps[1][:, 0:NC], 1.0, None, ALU.add))
                for k in range(2):
                    last = nc.vector.tensor_copy(deg[:, k, 0:NC], ps[k][:, 0:NC])
                step(last)
                dve.sem_inc(t_in.sem, 1)
                step(nc.vector.tensor_scalar(inv[:], deg[:, :, 0:NC], 1.0, None, ALU.max))
                nc.vector.reciprocal(dinv[:], dinv[:]).then_inc(y_ready.sem, 1)
                step(nc.vector.reciprocal(inv[:], inv[:]))
                step(nc.vector.tensor_scalar(invs[:], deg[:, :, 0:NC], 1.0, None, ALU.min))
                step(nc.vector.tensor_tensor(inv[:], inv[:], invs[:], ALU.mult))
                nc.vector.tensor_scalar(invs[:, 0, :], inv[:, 0, :], 1.0 / FIX, None, ALU.mult)
                dve.wait_ge(t_mm.sem, t_mm.at(1))
                step(nc.vector.tensor_copy(run[:, 0], ps[3][:, 0:NC + 1]))
                step(nc.vector.tensor_tensor_scan(run[:, 1], run[:, 0], run[:, 0], 0.0, ALU.add, ALU.bypass))
                step(nc.vector.tensor_tensor(run[:, 1], run[:, 1], run[:, 0], ALU.subtract))
                step(nc.vector.tensor_tensor(below, run[:, 1], ps[2][:, 0:NC + 1], ALU.add))
                dve.sem_inc(t_in.sem, 1)
                dve.wait_ge(t_tr.sem, t_tr.at(1))
                nc.vector.tensor_copy(belowT[0:NC + 1, :], ps[4][0:NC + 1, 0:P]).then_inc(t_cp.sem, 1)
                dve.wait_ge(ld2.sem, ld2.at(16 * 2 * NSB))
                nc.vector.tensor_copy(startf[:, 1, :], starts[:, 1, :])
                step(nc.vector.tensor_single_scalar(first, starts[:, 0, :], 3, ALU.logical_shift_right))
                dve.sem_inc(t_in.sem, 1)
                step(nc.vector.tensor_copy(startf[:, 0, :], first))
                step(nc.vector.scalar_tensor_tensor(startf[:, 1, :], startf[:, 0, :], -float(STEP), startf[:, 1, :],
                                                    ALU.mult, ALU.add))
                step(nc.vector.tensor_scalar(startf[:, 1, :], startf[:, 1, :], float(P), None, ALU.is_gt))
                step(nc.vector.tensor_reduce(bad[:, 1:2], startf[:, 1, :], AX.X, ALU.max))
                step(nc.vector.tensor_tensor(bad[:, 0:1], bad[:, 0:1], bad[:, 1:2], ALU.max))
                dve.sem_inc(t_in.sem, 1)
                dve.wait_ge(t_mm.sem, t_mm.at(2))
                step(nc.vector.tensor_scalar(flag[:], ps[5][:, 0:1], 1.0, None, ALU.min))
                dve.wait_ge(t_tr.sem, t_tr.at(2))
                step(nc.vector.tensor_copy(wbits[:, 0, 0:4 * P], ps[6][:, :]))
                step(nc.vector.tensor_copy(wbits[:, 0, 4 * P:5 * P], ps[7][:, 0:P]))
                nc.vector.tensor_single_scalar(wbits[:, 1], wbits[:, 0], 12, ALU.logical_shift_right)
                nc.vector.tensor_single_scalar(wbits[:, 2], wbits[:, 0], P - 1, ALU.bitwise_and)
                step(nc.vector.tensor_single_scalar(wbits[:, 3], wbits[:, 0], 7, ALU.logical_shift_right))
                nc.vector.tensor_copy(wf[:, 0], wbits[:, 1])
                nc.vector.tensor_copy(slo[:], wbits[:, 2])
                step(nc.vector.tensor_single_scalar(wbits[:, 0], wbits[:, 3], 31, ALU.bitwise_and))
                nc.vector.tensor_copy(wf[:, 1], wbits[:, 0])
                step(nc.vector.tensor_tensor(wf[:, 0], wf[:, 0], gbase, ALU.subtract))
                nc.vector.tensor_scalar(wf[:, 2], wf[:, 0], 0.0, None, ALU.is_lt)
                step(nc.vector.scalar_tensor_tensor(wf[:, 1], wf[:, 1], float(GN), wf[:, 0], ALU.mult, ALU.add))
                step(nc.vector.scalar_tensor_tensor(wf[:, 2], wf[:, 0], float(GN - 1), wf[:, 2], ALU.is_gt, ALU.add))
                step(nc.vector.scalar_tensor_tensor(rk[:], wf[:, 2], 65536.0, wf[:, 1], ALU.mult, ALU.add))
                ch.close(step.done)

            @block.tensor
            def _(pe):
                for k in range(2):
                    nc.tensor.matmul(ps[k][:, 0:NC], zero16[:, 0:P], zero16[:, 0:NC], start=True, stop=False)
                with pe.Fori(0, trips) as i:
                    pe.wait_ge(deg_lo.sem, i + 1)
                    for k in range(2):
                        for t in range(EB):
                            last = nc.tensor.matmul(ps[k][:, 0:NC], oh_lo[:, k, t, :], oh_hi[:, k, t, :],
                                                    start=False, stop=False)
                    last.then_inc(deg_mm.sem, 1)
                for k in range(2):
                    last = nc.tensor.matmul(ps[k][:, 0:NC], zero16[:, 0:P], zero16[:, 0:NC],
                                            start=False, stop=True)
                last.then_inc(deg_mm.sem, 1)
                pe.wait_ge(t_in.sem, t_in.at(1))
                nc.tensor.matmul(ps[2][:, 0:NC + 1], before[:], deg[:, 1, :], start=True, stop=True)
                nc.tensor.matmul(ps[3][:, 0:NC + 1], ones[:], deg[:, 1, :], start=True, stop=True
                                 ).then_inc(t_mm.sem, 1)
                pe.wait_ge(t_in.sem, t_in.at(2))
                nc.tensor.transpose(ps[4][0:NC + 1, 0:P], below, ident[:]).then_inc(t_tr.sem, 1)
                pe.wait_ge(t_in.sem, t_in.at(4))
                nc.tensor.matmul(ps[5][:, 0:1], ones[:], bad[:, 0:1], start=True, stop=True).then_inc(t_mm.sem, 1)
                pe.wait_ge(f_gx.sem, f_gx.at(16 * NSB))
                for b in range(NSB):
                    last = nc.tensor.transpose(ps[6 + b // 4][:, (b % 4) * P:(b % 4 + 1) * P], win[:, b, :], ident[:])
                last.then_inc(t_tr.sem, 1)

            @block.scalar
            def _(act):
                act.wait_ge(y_ready.sem, 2)
                nc.scalar.activation(dinv[:], dinv[:], ACT.Sqrt).then_inc(y_ready.sem, 1)

            @block.sync
            def _(sp):
                sp.wait_ge(y_ready.sem, 1)
                sp.dma_start(packed_dram[0:E].rearrange("(p j) -> p j", j=EW), key[0:ER, :]).then_inc(st.sem, 16)
                tail = WROWS * STEP + P - E
                sp.dma_start(packed_dram[E:E + tail].rearrange("(p j) -> p j", p=1), padkeys[0:1, 0:tail]
                             ).then_inc(st.sem, 16)
                sp.wait_ge(st.sem, st.at(32))
                flat = packed_dram
                over8 = bass.AP(tensor=flat.tensor, offset=flat.offset, ap=[[STEP, WROWS], [1, P]])
                sp.dma_start(window_dram, over8).then_inc(st2.sem, 16)
                sp.wait_ge(t_cp.sem, t_cp.at(1))
                sp.dma_start(below_dram.rearrange("(c p) -> c p", p=P), belowT[0:NC + 1, :]).then_inc(st.sem, 16)
                sp.wait_ge(st.sem, st.at(48))
                with nc.allow_non_contiguous_dma(reason="a number per group, once"):
                    for k in range(2):
                        for b in range(NSB):
                            at = GN * (b * P + k)
                            from_ = bass.AP(tensor=below_dram.tensor, offset=below_dram.offset + at,
                                            ap=[[GN, P], [1, 1]])
                            sp.dma_start(starts[:, k, b:b + 1], from_).then_inc(ld2.sem, 16)
                sp.wait_ge(ld2.sem, ld2.at(16 * 2 * NSB))

            @block.gpsimd
            def _(pool):
                pool.wait_ge(st2.sem, st2.at(16))
                pool.wait_ge(t_in.sem, t_in.at(3))
                for b in range(NSB):
                    pool.indirect_dma_start(
                        out=win[:, b, :], out_offset=None, in_=window_dram,
                        in_offset=bass.IndirectOffsetOnAxis(ap=first[:, b:b + 1], axis=0),
                        bounds_check=WROWS - 1, oob_is_err=False).then_inc(f_gx.sem, 16)
                pool.wait_ge(f_gx.sem, f_gx.at(16 * NSB))
        ld2.close(16 * 2 * NSB)
        f_gx.close(16 * NSB)
        t_in.close(4)
        t_mm.close(2)
        t_tr.close(2)
        t_cp.close(1)
        st.close(48)
        st2.close(16)

        ats = [BIG[:, k * NC * SB // 2:(k + 1) * NC * SB // 2].bitcast(F16).rearrange("p (c n) -> p c n", c=NC)
               for k in range(2)]
        arow = [SR[:, k * NP // 2:(k + 1) * NP // 2].bitcast(F16) for k in range(5)]
        ohs = wk[:, :, :].bitcast(F16).rearrange("p a (b t n) -> p (a b) t n", b=2, t=4)
        ohr = wn[:, :, :].bitcast(F16).rearrange("p a (b t n) -> p (a b) t n", b=2, t=4)
        QUADS = GROUPS // 4
        QB = QUADS // NSB
        NR = GN * NC
        ps16 = [ps[4 + k][:, 0:SB // 2].bitcast(F16) for k in range(4)]

        def superblocks(eng, emit):
            with eng.Fori(0, NSB // 2) as i:
                for k in range(2):
                    emit(i * 2 + k, k, i)
            emit(NSB - 1, (NSB - 1) % 2, NSB // 2)

        def general(eng):
            return eng.value_load(flag[0:1, 0:1], min_val=0, max_val=1)

        ON_ACT = (1, 3)

        def copy_rows(eng, copy, b, mine, counter):
            for j in range(5):
                eng.wait_ge(r_st[j].sem, r_st[j].at(16 * b))
                for f in mine:
                    m = j * 5 + f
                    eng.wait_ge(r_tr.sem, r_tr.at(b * 25 + m + 1))
                    copy(arow[j][:, f * SB:(f + 1) * SB], ps16[m % 4]).then_inc(counter.sem, 1)

        with nc.Block() as block:
            @block.vector
            def _(dve):
                with dve.If(general(dve)):
                    dve.nop()
                with dve.Else():
                    def emit(b, buf, uses):
                        with dve.Fori(0, QB // 4) as i:
                            for u in range(4):
                                q = b * QB + i * 4 + u
                                dve.wait_ge(q_mm.sem, q_mm.at(q - 3))
                                for t in range(4):
                                    g = bass.ds(q * 4 + t, 1)
                                    nc.vector.tensor_scalar(ohs[:, u, t, :], iota16[:, :], slo[:, g], None, ALU.is_equal)
                                    last = nc.vector.tensor_scalar(ohr[:, u, t, 0:NR], iota16[:, 0:NR], rk[:, g],
                                                                   None, ALU.is_equal)
                                last.then_inc(q_in.sem, 1)
                        copy_rows(dve, nc.vector.tensor_copy, b, [f for f in range(5) if f not in ON_ACT], r_dve)
                    superblocks(dve, emit)

            @block.scalar
            def _(act):
                with act.If(general(act)):
                    act.nop()
                with act.Else():
                    def emit(b, buf, uses):
                        act.wait_ge(s_st[buf].sem, s_st[buf].at(16 * uses))
                        act.wait_ge(r_tr.sem, r_tr.at(b * 25 - 25))
                        with act.Fori(0, QB // 4) as i:
                            for u in range(4):
                                q = b * QB + i * 4 + u
                                act.wait_ge(q_mm.sem, q_mm.at(q + 1))
                                to = ats[buf][:, :, bass.ds(i * 80 + u * 20, 20)].rearrange("p c (t n) -> p t c n", n=GN)
                                nc.scalar.copy(to, ps[u][:, 0:4 * NR].rearrange("p (t c n) -> p t c n", t=4, c=NC)
                                               ).then_inc(q_ev.sem, 1)
                        copy_rows(act, nc.scalar.copy, b, list(ON_ACT), r_act)
                    superblocks(act, emit)

            @block.tensor
            def _(pe):
                with pe.If(general(pe)):
                    pe.nop()
                with pe.Else():
                    def emit(b, buf, uses):
                        with pe.Fori(0, QB // 4) as i:
                            for u in range(4):
                                q = b * QB + i * 4 + u
                                pe.wait_ge(q_in.sem, q_in.at(q + 1))
                                pe.wait_ge(q_ev.sem, q_ev.at(q - 3))
                                for t in range(4):
                                    last = nc.tensor.matmul(ps[u][:, t * NR:(t + 1) * NR], ohs[:, u, t, :],
                                                            ohr[:, u, t, 0:NR], start=True, stop=True)
                                last.then_inc(q_mm.sem, 1)
                        pe.wait_ge(q_ev.sem, q_ev.at(b * QB + QB))
                        for m in range(25):
                            j, f = divmod(m, 5)
                            done = m - 3 if m else 0
                            on_act = sum(1 for x in range(max(done, 0)) if x % 5 in ON_ACT)
                            pe.wait_ge(r_act.sem, r_act.at(b * 10 + (on_act if m else 0)))
                            pe.wait_ge(r_dve.sem, r_dve.at(b * 15 + (max(done, 0) - on_act if m else 0)))
                            for x in range(5):
                                last = nc.tensor.transpose(ps16[m % 4][:, x * P:(x + 1) * P],
                                                           ats[buf][:, f * 5 + x, j * P:(j + 1) * P], ident16[:])
                            last.then_inc(r_tr.sem, 1)
                    superblocks(pe, emit)

            @block.sync
            def _(sp):
                with sp.If(general(sp)):
                    sp.nop()
                with sp.Else():
                    def emit(b, buf, uses):
                        sp.wait_ge(q_ev.sem, q_ev.at(b * QB + QB))
                        sp.dma_start(at_dram.rearrange("(c p) n -> p c n", p=P)[:, :, bass.ds(b * SB, SB)], ats[buf]
                                     ).then_inc(s_st[buf].sem, 16)
                        for j in range(5):
                            sp.wait_ge(r_act.sem, r_act.at(b * 10 + 2 * j + 2))
                            sp.sem_inc(s_gate.sem, 1)
                            sp.wait_ge(r_dve.sem, r_dve.at(b * 15 + 3 * j + 3))
                            sp.dma_start(a_dram[bass.ds(b * SB + j * P, P), :], arow[j]).then_inc(r_st[j].sem, 16)
                    superblocks(sp, emit)
                    for k, n in ((0, 3), (1, 2)):
                        sp.wait_ge(s_st[k].sem, s_st[k].at(16 * n))
                    for j in range(5):
                        sp.wait_ge(r_st[j].sem, r_st[j].at(16 * NSB))

        def row(t3, c):
            return t3[:, bass.ds(c, 1), 0:F].rearrange("p a f -> p (a f)")

        with nc.Block() as block:
            @block.vector
            def _(dve):
                nc.vector.tensor_scalar(dinvs[:], dinv[:], 1.0 / FIX, None, ALU.mult)

        def normalise():
            with nc.Block() as block:
                @block.vector
                def _(dve):
                    step = Chain(dve, ch)
                    with dve.Fori(0, NC) as c:
                        nc.vector.bn_stats(bnbuf[:, bass.ds(c, 1), :].rearrange("p a f -> p (a f)"), row(XR, c)
                                           ).then_inc(t_out.sem, 1)
                    dve.wait_ge(t_out.sem, t_out.at(NC))
                    for c in range(NC):
                        last = nc.vector.bn_aggr(stats[:, c, :], bnbuf[:, c, :])
                    step(last)
                    step(nc.vector.tensor_scalar(rstd[:], stats[:, :, 1], EPS, None, ALU.add))
                    nc.vector.reciprocal(rstd[:], rstd[:]).then_inc(t_in.sem, 1)
                    dve.wait_ge(t_cp.sem, t_cp.at(1))
                    with dve.Fori(0, NC) as c:
                        one = bass.ds(c, 1)
                        nc.vector.tensor_scalar(
                            Z[:, one, 0:F].rearrange("p a f -> p (a f)"),
                            XR[:, one, :].rearrange("p a f -> p (a f)"),
                            stats[:, one, 0:1].rearrange("p a f -> p (a f)"),
                            rstd[:, one], ALU.subtract, ALU.mult)
                    ch.close(step.done)

                @block.scalar
                def _(act):
                    act.wait_ge(t_in.sem, t_in.at(1))
                    nc.scalar.activation(rstd[:], rstd[:], ACT.Sqrt).then_inc(t_cp.sem, 1)
            t_in.close(1)
            t_cp.close(1)
            t_out.close(NC)

        XH = BIG[:, 0:NC * F].bitcast(F16).rearrange("p (c f) -> p c f", c=NC)
        MB = BIG[:, NC * F:NC * F + 5 * 5 * SB // 2].bitcast(F16).rearrange("p (k c n) -> p k c n", k=5, c=5)

        def sum_over_edges(a, b, matrix, produce):
            S5 = S.rearrange("p (g c) f -> p g (c f)", c=5)
            with nc.Block() as block:
                @block.vector
                def _(dve):
                    with dve.If(general(dve)):
                        step = Chain(dve, chg)
                        with dve.Fori(0, NC) as c:
                            last = produce(c)
                            last.then_inc(f_src.sem, 1)
                        with dve.Fori(0, ET) as j:
                            step.enter(j, 4)
                            one = bass.ds(j, 1)
                            dve.wait_ge(f_put.sem, f_put.at(16 * NC + j * 16))
                            nc.vector.tensor_copy(fix[:, 0:1], ids[:, b, one])
                            nc.vector.tensor_scalar(gix[:, 0:1], ids[:, a, one], float(NP - 1), None, ALU.min)
                            nc.vector.tensor_scalar(gix[:, 1:2], ids[:, b, one], float(NP - 1), None, ALU.min)
                            step(nc.vector.tensor_copy(wk[:, 0, 0:P], ids[:, b, one].to_broadcast([P, P])))
                            dve.sem_inc(f_idx.sem, 1)
                            dve.wait_ge(f_row.sem, f_row.at(j + 1))
                            step(nc.vector.tensor_scalar(wk[:, 0, P:2 * P], ps[0][:, 0:P], fix[:, 0:1], None,
                                                         ALU.is_equal))
                            nc.vector.tensor_tensor(wn[:, 0, 0:P], wk[:, 0, P:2 * P], after[:], ALU.mult
                                                    ).then_inc(f_eq.sem, 1)
                            dve.wait_ge(f_eq.sem, f_eq.at(j + 1))
                            step(nc.vector.tensor_reduce(fix[:, 1:2], wn[:, 0, 0:P], AX.X, ALU.add))
                            step(nc.vector.scalar_tensor_tensor(gix[:, 2:3], fix[:, 1:2], float(2 * PAD_NODE),
                                                                fix[:, 0:1], ALU.mult, ALU.add))
                            dve.wait_ge(f_ga.sem, f_ga.at(16 * (j + 1)))
                            dve.wait_ge(f_mm.sem, f_mm.at(j + 1))
                            nc.vector.tensor_tensor(tT[:, 0, :], tb[:, 1, :], ps[1][:, 0:F], ALU.add
                                                    ).then_inc(f_add.sem, 1)
                        step.leave(ET)
                        chg.close(step.done)
                    with dve.Else():
                        step = Chain(dve, ch)
                        with dve.Fori(0, NC // 5) as g:
                            step.enter(g, 2)
                            for k in range(5):
                                last = produce(g * 5 + k)
                            step(last)
                            one = bass.ds(g, 1)
                            rows = S5[:, one, :].rearrange("p a (c f) -> p (a c) f", f=F)
                            step(nc.vector.tensor_copy(XH[:, bass.ds(g * 5, 5), 0:F], rows))
                            nc.vector.tensor_tensor(XH[:, bass.ds(g * 5, 5), F:2 * F], rows,
                                                    XH[:, bass.ds(g * 5, 5), 0:F], ALU.subtract).then_inc(a_in.sem, 1)
                        step.leave(NC // 5)
                        with dve.Fori(0, NC // 5) as g:
                            for j in range(5):
                                n = g * 5 + j
                                dve.wait_ge(a_lo.sem, a_lo.at(n + 1))
                                nc.vector.tensor_tensor(row(R, n), ps[j][:, 0:F], wk[:, j % 2, 0:F], ALU.add
                                                        ).then_inc(a_ev.sem, 1)
                        ch.close(step.done)

                @block.scalar
                def _(act):
                    with act.If(general(act)):
                        act.nop()
                    with act.Else():
                        with act.Fori(0, NC // 5) as g:
                            for j in range(5):
                                n = g * 5 + j
                                act.wait_ge(a_mm.sem, a_mm.at(n + 1))
                                act.wait_ge(a_ev.sem, a_ev.at(n + early(j)))
                                nc.scalar.copy(wk[:, j % 2, 0:F], ps[j][:, F:2 * F]).then_inc(a_lo.sem, 1)

                @block.tensor
                def _(pe):
                    with pe.If(general(pe)):
                        with pe.Fori(0, ET) as j:
                            pe.wait_ge(f_idx.sem, f_idx.at(j + 1))
                            nc.tensor.matmul(ps[0][:, 0:P], wk[:, 0, 0:P], ident[:], start=True, stop=True
                                             ).then_inc(f_row.sem, 1)
                            pe.wait_ge(f_eq.sem, f_eq.at(j + 1))
                            pe.wait_ge(f_gx.sem, f_gx.at(16 * (j + 1)))
                            nc.tensor.matmul(ps[1][:, 0:F], wk[:, 0, P:2 * P], tb[:, 0, :], start=True, stop=True
                                             ).then_inc(f_mm.sem, 1)
                    with pe.Else():
                        with pe.Fori(0, NSB) as g:
                            for k in range(5):
                                pe.wait_ge(a_ld[k].sem, a_ld[k].at(16 * g + 16))
                                pe.wait_ge(a_in.sem, a_in.at(k + 1))
                                for j in range(5):
                                    if k == 0:
                                        pe.wait_ge(a_ev.sem, a_ev.at(g * 5 + j - 4))
                                    for c in range(5):
                                        last = nc.tensor.matmul(ps[j][:, :], MB[:, k, c, j * P:(j + 1) * P],
                                                                XH[:, k * 5 + c, :], start=(k == 0 and c == 0),
                                                                stop=(k == 4 and c == 4))
                                    if k == 4:
                                        last.then_inc(a_mm.sem, 1)
                                if k < 4:
                                    last.then_inc(a_kb.sem, 1)

                @block.sync
                def _(sp):
                    with sp.If(general(sp)):
                        sp.wait_ge(f_src.sem, f_src.at(NC))
                        sp.dma_start(agg_in_dram.rearrange("(c p) f -> p c f", p=P), S).then_inc(f_st.sem, 16)
                        sp.wait_ge(f_put.sem, f_put.at(16 * NC + 16 * ET))
                        sp.dma_start(R, agg_out_dram.rearrange("(c p) f -> p c f", p=P)).then_inc(f_ld.sem, 16)
                        sp.wait_ge(f_ld.sem, f_ld.at(16))
                    with sp.Else():
                        with sp.Fori(0, NSB) as g:
                            for k in range(5):
                                if k < 4:
                                    sp.wait_ge(a_kb.sem, a_kb.at(g * 4 + k - 3))
                                else:
                                    sp.wait_ge(a_mm.sem, a_mm.at(g * 5))
                                sp.dma_start(MB[:, k, :, :],
                                             matrix.rearrange("(k c p) n -> k p c n", c=5, p=P)[k][:, :, bass.ds(g * SB, SB)]
                                             ).then_inc(a_ld[k].sem, 16)

                @block.gpsimd
                def _(pool):
                    with pool.If(general(pool)):
                        for c in range(NC):
                            pool.dma_start(agg_out_dram[c * P:(c + 1) * P, :], zeros[:, 0:F]).then_inc(f_put.sem, 16)
                        limit = pool.to_reg(NP - 1)
                        pool.wait_ge(f_put.sem, f_put.at(16 * NC))
                        pool.wait_ge(f_st.sem, f_st.at(16))
                        with pool.Fori(0, ET) as j:
                            pool.wait_ge(f_idx.sem, f_idx.at(j + 1))
                            pool.sem_inc(gate.sem, 1)
                            pool.indirect_dma_start(
                                out=tb[:, 0, :], out_offset=None, in_=agg_in_dram,
                                in_offset=bass.IndirectOffsetOnAxis(ap=gix[:, 0:1], axis=0),
                                bounds_check=limit, oob_is_err=False).then_inc(f_gx.sem, 16)
                            pool.indirect_dma_start(
                                out=tb[:, 1, :], out_offset=None, in_=agg_out_dram,
                                in_offset=bass.IndirectOffsetOnAxis(ap=gix[:, 1:2], axis=0),
                                bounds_check=limit, oob_is_err=False).then_inc(f_ga.sem, 16)
                            pool.wait_ge(f_add.sem, f_add.at(j + 1))
                            pool.sem_inc(gate.sem, 1)
                            pool.indirect_dma_start(
                                out=agg_out_dram, in_=tT[:, 0, :], in_offset=None,
                                out_offset=bass.IndirectOffsetOnAxis(ap=gix[:, 2:3], axis=0),
                                bounds_check=limit, oob_is_err=False).then_inc(f_put.sem, 16)
                        pool.wait_ge(f_put.sem, f_put.at(16 * NC + 16 * ET))
                    with pool.Else():
                        pool.nop()
            for t, k in ((f_idx, ET), (f_row, ET), (f_eq, ET), (f_mm, ET), (f_add, ET),
                         (f_gx, 16 * ET), (f_ga, 16 * ET), (f_put, 16 * NC + 16 * ET), (f_src, NC),
                         (f_st, 16), (f_ld, 16),
                         (a_in, 5), (a_mm, NC), (a_lo, NC), (a_ev, NC), (a_kb, 4 * NSB), *((t, 16 * NSB) for t in a_ld)):
                t.close(k)

        def early(j):
            return -1 if j else 0

        def graph_product(kw, prepare, steps_in, consume, steps_out):
            with nc.Block() as block:
                @block.vector
                def _(dve):
                    step = Chain(dve, ch)
                    per = U * (steps_in + steps_out)
                    with dve.Fori(0, NC // U) as i:
                        step.enter(i, per)
                        for j in range(U):
                            n = i * U + j
                            dve.wait_ge(t_tr.sem, t_tr.at(n + early(j)))
                            prepare(dve, step, n, tb[:, j % 2, :])
                            dve.sem_inc(t_in.sem, 1)
                            dve.wait_ge(t_mm.sem, t_mm.at(n + 1))
                            consume(dve, step, n, ps[2 + j % 2][:, 0:F])
                            dve.sem_inc(t_out.sem, 1)
                    step.leave(NC // U)
                    ch.close(step.done)

                @block.scalar
                def _(act):
                    with act.Fori(0, NC // U) as i:
                        for j in range(U):
                            n = i * U + j
                            act.wait_ge(t_tr.sem, t_tr.at(n + 1))
                            act.wait_ge(t_mm.sem, t_mm.at(n + early(j)))
                            nc.scalar.copy(tT[:, j % 2, :], ps[j % 2][:, 0:F]).then_inc(t_cp.sem, 1)

                @block.tensor
                def _(pe):
                    with pe.Fori(0, NC // U) as i:
                        for j in range(U):
                            n = i * U + j
                            pe.wait_ge(t_in.sem, t_in.at(n + 1))
                            pe.wait_ge(t_cp.sem, t_cp.at(n + early(j)))
                            for k in range(KF):
                                last = nc.tensor.transpose(ps[j % 2][:, k * P:(k + 1) * P],
                                                           tb[:, j % 2, k * P:(k + 1) * P], ident[:])
                            last.then_inc(t_tr.sem, 1)
                            pe.wait_ge(t_cp.sem, t_cp.at(n + 1))
                            pe.wait_ge(t_out.sem, t_out.at(n + early(j)))
                            for k in range(KF):
                                last = nc.tensor.matmul(ps[2 + j % 2][:, 0:F], tT[:, j % 2, k * P:(k + 1) * P],
                                                        gw[:, kw, k, :], start=(k == 0), stop=(k == KF - 1))
                            last.then_inc(t_mm.sem, 1)
            for t in (t_in, t_tr, t_cp, t_mm, t_out):
                t.close(NC)

        normalise()

        def from_z(scale):
            def produce(c):
                if scale is None:
                    return nc.vector.tensor_scalar(row(S, c), row(Z, c), FIX, None, ALU.mult)
                return nc.vector.tensor_scalar(row(S, c), row(Z, c), scale[:, bass.ds(c, 1)], FIX, ALU.mult, ALU.mult)
            return produce

        def mean_of_sums(c):
            return nc.vector.tensor_scalar(row(S, c), row(R, c), inv[:, 1, bass.ds(c, 1)], None, ALU.mult)

        def scaled_h(c):
            return nc.vector.tensor_scalar(row(S, c), row(S, c), hmax[:, NC + 2:NC + 3], None, ALU.mult)

        sum_over_edges(0, 1, at_dram, from_z(dinv))

        def take_sum(dve, step, c, dst_tile):
            step(nc.vector.tensor_tensor(dst_tile, row(R, c), row(S, c), ALU.add))

        def put_l0(dve, step, c, prod):
            step(nc.vector.scalar_tensor_tensor(wk[:, 0, 0:F], prod, dinvs[:, bass.ds(c, 1)], bias[:, 0, :],
                                                ALU.mult, ALU.add))
            step(nc.vector.scalar_tensor_tensor(row(XR, c), wk[:, 0, 0:F], 0.0, row(XR, c), ALU.max, ALU.add))

        graph_product(0, take_sum, 1, put_l0, 2)
        normalise()

        wx = BIG[:, 0:KF * INNER].rearrange("p (k n) -> p k n", k=KF)
        wfx = BIG[:, 1024:1024 + KF * INNER].rearrange("p (k n) -> p k n", k=KF)
        wo = BIG[:, 2048:2048 + NPAIR * F].rearrange("p (t f) -> p t f", t=NPAIR)
        wxT = BIG[:, 3072:3072 + NPAIR * F].rearrange("p (t f) -> p t f", t=NPAIR)
        wxs = BIG[:, 4096:4096 + KF * INNER].rearrange("p (k n) -> p k n", k=KF)
        two = BIG[:, 5120:5120 + 4 * P].rearrange("p (k n) -> p k n", k=4)
        bxs = BIG[:, 5632:5632 + INNER]
        bfx = BIG[:, 6144:6144 + INNER]
        bcol = BIG[:, 6656:6656 + NPAIR]
        it = BIG[:, 6660:6660 + H]
        colb = BIG[:, 6784:6784 + INNER].rearrange("p (t m) -> p t m", t=NPAIR)
        bsl = BIG[:, 7296:7296 + G]
        with nc.Block() as block:
            @block.sync
            def _(sp):
                sp.wait_ge(cst.sem, cst.at(1))
                sp.dma_start(wx, w_x.rearrange("(k p) n -> p k n", p=P)).then_inc(ld.sem, 16)
                sp.dma_start(wfx, w_fx.rearrange("(k p) n -> p k n", p=P)).then_inc(ld.sem, 16)
                sp.dma_start(wo, w_out.rearrange("(t p) f -> p t f", p=P)).then_inc(ld.sem, 16)
                sp.dma_start(bfx, b_fx.partition_broadcast(P)).then_inc(ld.sem, 16)
                with nc.allow_non_contiguous_dma(reason="a bias as columns, once"):
                    sp.dma_start(bcol, b_x.rearrange("(t p) -> p t", p=P)).then_inc(ld.sem, 16)
                sp.dma_start(it, temperature.rearrange("a h b c -> (a h b c)").partition_broadcast(P)
                             ).then_inc(ld.sem, 16)
                sp.dma_start(bsl, b_slice.partition_broadcast(P)).then_inc(ld.sem, 16)
                for k, w in enumerate((w_slice, w_q, w_k, w_v)):
                    for h in range(2):
                        sp.dma_start(two[h * 64:h * 64 + 64, k, h * 64:h * 64 + 64], w).then_inc(ld.sem, 16)
                sp.wait_ge(ld.sem, ld.at(16 * 15))

            @block.gpsimd
            def _(pool):
                pool.memset(two, 0.0).then_inc(cst.sem, 1)
        ld.close(16 * 15)
        cst.close(1)
        with nc.Block() as block:
            @block.tensor
            def _(pe):
                for t in range(NPAIR):
                    for k in range(KF):
                        last = nc.tensor.transpose(ps[t % 2][:, (2 * (t // 2) + k) * P:(2 * (t // 2) + k + 1) * P],
                                                   wx[:, k, t * P:(t + 1) * P], ident[:])
                last.then_inc(t_tr.sem, 1)
                pe.wait_ge(t_cp.sem, t_cp.at(1))
                for k in range(KF):
                    for t in range(NPAIR):
                        nc.tensor.matmul(ps[2 + k][:, t * P:(t + 1) * P], wxT[:, t, k * P:(k + 1) * P],
                                         two[:, 0, :], start=True, stop=True)
                for t in range(NPAIR):
                    last = nc.tensor.matmul(ps[4][:, t * P:(t + 1) * P], colb[:, t, :], two[:, 0, :],
                                            start=True, stop=True)
                last.then_inc(t_mm.sem, 1)

            @block.vector
            def _(dve):
                step = Chain(dve, ch)
                step(nc.vector.tensor_scalar(it, it, 0.1, 5.0, ALU.max, ALU.min))
                step(nc.vector.reciprocal(it, it))
                nc.vector.tensor_copy(colb, bcol.unsqueeze(2).to_broadcast([P, NPAIR, P]))
                dve.wait_ge(t_tr.sem, t_tr.at(1))
                for t in range(NPAIR):
                    last = nc.vector.tensor_copy(wxT[:, t, :], ps[t % 2][:, (t // 2) * F:(t // 2) * F + F])
                last.then_inc(t_cp.sem, 1)
                dve.wait_ge(t_mm.sem, t_mm.at(1))
                it3 = it.unsqueeze(2).to_broadcast([P, H, G])
                for k in range(KF):
                    nc.vector.tensor_tensor(wxs[:, k, :].rearrange("p (h g) -> p h g", h=H),
                                            ps[2 + k][:, :].rearrange("p (h g) -> p h g", h=H), it3, ALU.mult)
                b3 = bxs.rearrange("p (h g) -> p h g", h=H)
                step(nc.vector.tensor_tensor(b3, ps[4][:, :].rearrange("p (h g) -> p h g", h=H),
                                             bsl.unsqueeze(1).to_broadcast([P, H, G]), ALU.add))
                step(nc.vector.tensor_tensor(b3, b3, it3, ALU.mult))
                ch.close(step.done)
        for t in (t_tr, t_cp, t_mm):
            t.close(1)

        def heads(t2):
            return t2.rearrange("p (h g) -> p h g", h=H)

        with nc.Block() as block:
            @block.vector
            def _(dve):
                step = Chain(dve, ch)
                per = U * 7
                with dve.Fori(0, NC // U) as i:
                    step.enter(i, per)
                    for j in range(U):
                        n, b = i * U + j, j % 2
                        dve.wait_ge(t_tr.sem, t_tr.at(n + early(j)))
                        nc.vector.tensor_copy(tb[:, b, :], row(Z, n)).then_inc(t_in.sem, 1)
                        dve.wait_ge(t_mm.sem, t_mm.at(n + 1))
                        step(nc.vector.tensor_tensor(wk[:, b, :], ps[2 + b][:, :], bxs, ALU.add))
                        dve.sem_inc(t_out.sem, 1)
                        mx, sx = sm[:, b, 0:H], sm[:, b, H:2 * H]
                        step(nc.vector.tensor_reduce(mx, heads(wk[:, b, :]), AX.X, ALU.max))
                        step(nc.vector.tensor_tensor(heads(wk[:, b, :]), heads(wk[:, b, :]),
                                                     mx.unsqueeze(2).to_broadcast([P, H, G]), ALU.subtract))
                        dve.sem_inc(m_mm.sem, 1)
                        dve.wait_ge(m_out.sem, m_out.at(n + 1))
                        step(nc.vector.tensor_reduce(sx, heads(wk[:, b, :]), AX.X, ALU.add))
                        step(nc.vector.reciprocal(sx, sx))
                        step(nc.vector.tensor_scalar(sx, sx, valid[:, bass.ds(n, 1)], None, ALU.mult))
                        dve.wait_ge(n_a.sem, n_a.at(n + early(j)))
                        step(nc.vector.tensor_tensor(heads(wn[:, b, :]), heads(wk[:, b, :]),
                                                     sx.unsqueeze(2).to_broadcast([P, H, G]), ALU.mult))
                        dve.sem_inc(n_b.sem, 1)
                step.leave(NC // U)
                ch.close(step.done)

            @block.scalar
            def _(act):
                with act.Fori(0, NC // U) as i:
                    for j in range(U):
                        n, b = i * U + j, j % 2
                        act.wait_ge(t_tr.sem, t_tr.at(n + 1))
                        act.wait_ge(t_mm.sem, t_mm.at(n + early(j)))
                        nc.scalar.copy(tT[:, b, :], ps[b][:, 0:F]).then_inc(t_cp.sem, 1)
                        act.wait_ge(m_mm.sem, m_mm.at(n + 1))
                        nc.scalar.activation(wk[:, b, :], wk[:, b, :], ACT.Exp).then_inc(m_out.sem, 1)
                        act.wait_ge(m_tr.sem, m_tr.at(n + 1))
                        nc.scalar.copy(WT[:, bass.ds(n, 1), :].rearrange("p a k -> p (a k)"), ps[b][:, :]
                                       ).then_inc(m_cp.sem, 1)

            @block.tensor
            def _(pe):
                for t in range(NPAIR):
                    nc.tensor.matmul(ps[4 + t][:, 0:F + 4], zeros[:, 0:P], zeros[:, 0:F + 4], start=True, stop=False)
                with pe.Fori(0, NC // U) as i:
                    for j in range(U):
                        n, b = i * U + j, j % 2
                        pe.wait_ge(t_in.sem, t_in.at(n + 1))
                        pe.wait_ge(m_cp.sem, m_cp.at(n + early(j)))
                        for k in range(KF):
                            last = nc.tensor.transpose(ps[b][:, k * P:(k + 1) * P], tb[:, b, k * P:(k + 1) * P],
                                                       ident[:])
                        last.then_inc(t_tr.sem, 1)
                        pe.wait_ge(t_cp.sem, t_cp.at(n + 1))
                        pe.wait_ge(t_out.sem, t_out.at(n + early(j)))
                        for k in range(KF):
                            last = nc.tensor.matmul(ps[2 + b][:, :], tT[:, b, k * P:(k + 1) * P], wxs[:, k, :],
                                                    start=(k == 0), stop=(k == KF - 1))
                        last.then_inc(t_mm.sem, 1)
                        pe.wait_ge(n_b.sem, n_b.at(n + 1))
                        for t in range(NPAIR):
                            last = nc.tensor.transpose(ps[b][:, t * P:(t + 1) * P], wn[:, b, t * P:(t + 1) * P],
                                                       ident[:])
                        last.then_inc(m_tr.sem, 1)
                        for t in range(NPAIR):
                            last = nc.tensor.matmul(ps[4 + t][:, 0:F + 4], wn[:, b, t * P:(t + 1) * P],
                                                    Z[:, bass.ds(n, 1), :].rearrange("p a f -> p (a f)"),
                                                    start=False, stop=False)
                        last.then_inc(n_a.sem, 1)
                for t in range(NPAIR):
                    last = nc.tensor.matmul(ps[4 + t][:, 0:F + 4], zeros[:, 0:P], zeros[:, 0:F + 4], start=False, stop=True)
                last.then_inc(n_a.sem, 1)
                pe.wait_ge(n_a.sem, n_a.at(NC + 1))
        for t in (t_in, t_tr, t_cp, t_mm, t_out, m_tr, m_cp, m_mm, m_out, n_b):
            t.close(NC)
        n_a.close(NC + 1)

        big0 = 7424
        xw = BIG[:, big0:big0 + NPAIR * (F + 4)].rearrange("p (t f) -> p t f", t=NPAIR)
        big1 = big0 + NPAIR * (F + 4)
        xwT = BIG[:, big1:big1 + KF * INNER].rearrange("p (k n) -> p k n", k=KF)
        big2 = big1 + KF * INNER
        tok, tokT, qT, kT, vT, att, attT = (
            BIG[:, big2 + m * INNER:big2 + (m + 1) * INNER].rearrange("p (t n) -> p t n", t=NPAIR) for m in range(7))
        big3 = big2 + 7 * INNER
        vo = BIG[:, big3:big3 + NPAIR * F].rearrange("p (t f) -> p t f", t=NPAIR)
        om = BIG[:, big3 + NPAIR * F:big3 + 2 * NPAIR * F].rearrange("p (t f) -> p t f", t=NPAIR)
        small = BIG[:, big3 + 2 * NPAIR * F:big3 + 2 * NPAIR * F + 16].rearrange("p (a t) -> p a t", t=NPAIR)
        assert big3 + 2 * NPAIR * F + 16 <= 2 * KH * X * F
        halves = [(0, slice(0, 64)), (1, slice(64, 128))]
        with nc.Block() as block:
            @block.vector
            def _(dve):
                step = Chain(dve, ch)
                for t in range(NPAIR):
                    nc.vector.tensor_copy(xw[:, t, :], ps[4 + t][:, 0:F + 4])
                nc.vector.memset(tok, 0.0)
                step(nc.vector.memset(att, 0.0))
                dve.sem_inc(t_in.sem, 1)
                dve.wait_ge(t_tr.sem, t_tr.at(1))
                for k in range(KF):
                    last = nc.vector.tensor_copy(xwT[:, k, :], ps[k][:, :])
                last.then_inc(t_cp.sem, 1)
                step(nc.vector.tensor_scalar(small[:, 0, :], xw[:, :, F], EPS, None, ALU.add))
                step(nc.vector.reciprocal(small[:, 0, :], small[:, 0, :]))
                dve.wait_ge(t_mm.sem, t_mm.at(1))
                for t in range(NPAIR):
                    for h, r in halves:
                        at = slice(t * P + 64 * h, t * P + 64 * h + 64)
                        last = nc.vector.scalar_tensor_tensor(tok[r, t, r], bfx[r, at], xw[r, t, F:F + 1],
                                                              ps[2][r, at], ALU.mult, ALU.add)
                step(last)
                for t in range(NPAIR):
                    last = nc.vector.tensor_scalar(tok[:, t, :], tok[:, t, :], small[:, 0, t:t + 1], None, ALU.mult)
                step(last)
                dve.sem_inc(t_in.sem, 1)
                dve.wait_ge(t_tr.sem, t_tr.at(2))
                nc.vector.tensor_copy(tokT, ps[0][:, :].rearrange("p (t n) -> p t n", t=NPAIR)).then_inc(t_cp.sem, 1)
                dve.wait_ge(t_mm.sem, t_mm.at(2))
                for m, to in ((1, qT), (2, kT), (3, vT)):
                    last = nc.vector.tensor_copy(to, ps[m][:, :].rearrange("p (t n) -> p t n", t=NPAIR))
                last.then_inc(t_cp.sem, 1)
                dve.wait_ge(t_mm.sem, t_mm.at(3))
                for t in range(NPAIR):
                    for h, r in halves:
                        last = nc.vector.tensor_reduce(small[r, 1, t:t + 1], ps[4][r, t * P + 64 * h:t * P + 64 * h + 64],
                                                       AX.X, ALU.max)
                step(last)
                step(nc.vector.tensor_scalar(small[:, 1, :], small[:, 1, :], -float(D) ** -0.5, None, ALU.mult))
                dve.sem_inc(m_mm.sem, 1)
                dve.wait_ge(m_out.sem, m_out.at(NPAIR * 2))
                step(nc.vector.reciprocal(small[:, 2, :], small[:, 2, :]))
                for t in range(NPAIR):
                    last = nc.vector.tensor_scalar(att[:, t, :], att[:, t, :], small[:, 2, t:t + 1], None, ALU.mult)
                step(last)
                dve.sem_inc(t_in.sem, 1)
                dve.wait_ge(t_tr.sem, t_tr.at(3))
                nc.vector.tensor_copy(attT, ps[0][:, :].rearrange("p (t n) -> p t n", t=NPAIR))
                dve.wait_ge(t_mm.sem, t_mm.at(4))
                for t in range(NPAIR):
                    last = nc.vector.tensor_copy(vo[:, t, :], ps[5 + t // 2][:, (t % 2) * F:(t % 2) * F + F])
                last.then_inc(t_cp.sem, 1)
                dve.wait_ge(t_mm.sem, t_mm.at(5))
                for t in range(NPAIR):
                    last = nc.vector.tensor_copy(om[:, t, :], ps[2 + t // 2][:, (t % 2) * F:(t % 2) * F + F])
                step(last)
                ch.close(step.done)

            @block.scalar
            def _(act):
                act.wait_ge(m_mm.sem, m_mm.at(1))
                for t in range(NPAIR):
                    for h, r in halves:
                        nc.scalar.activation(att[r, t, r], ps[4][r, t * P + 64 * h:t * P + 64 * h + 64], ACT.Exp,
                                             bias=small[r, 1, t:t + 1], scale=float(D) ** -0.5,
                                             accum_out=small[r, 2, t:t + 1]).then_inc(m_out.sem, 1)

            @block.tensor
            def _(pe):
                pe.wait_ge(t_in.sem, t_in.at(1))
                for k in range(KF):
                    for t in range(NPAIR):
                        last = nc.tensor.transpose(ps[k][:, t * P:(t + 1) * P], xw[:, t, k * P:(k + 1) * P], ident[:])
                last.then_inc(t_tr.sem, 1)
                pe.wait_ge(t_cp.sem, t_cp.at(1))
                for t in range(NPAIR):
                    for k in range(KF):
                        last = nc.tensor.matmul(ps[2][:, t * P:(t + 1) * P], xwT[:, k, t * P:(t + 1) * P],
                                                wfx[:, k, t * P:(t + 1) * P], start=(k == 0), stop=(k == KF - 1))
                last.then_inc(t_mm.sem, 1)
                pe.wait_ge(t_in.sem, t_in.at(2))
                for t in range(NPAIR):
                    last = nc.tensor.transpose(ps[0][:, t * P:(t + 1) * P], tok[:, t, :], ident[:])
                last.then_inc(t_tr.sem, 1)
                pe.wait_ge(t_cp.sem, t_cp.at(2))
                for m in (1, 2, 3):
                    last = nc.tensor.matmul(ps[m][:, :], two[:, m, :], tokT.rearrange("p t n -> p (t n)"),
                                            start=True, stop=True)
                last.then_inc(t_mm.sem, 1)
                pe.wait_ge(t_cp.sem, t_cp.at(3))
                for t in range(NPAIR):
                    last = nc.tensor.matmul(ps[4][:, t * P:(t + 1) * P], qT[:, t, :], kT[:, t, :], start=True, stop=True)
                last.then_inc(t_mm.sem, 1)
                for t in range(NPAIR):
                    last = nc.tensor.matmul(ps[5 + t // 2][:, (t % 2) * F:(t % 2) * F + F], vT[:, t, :], wo[:, t, :],
                                            start=True, stop=True)
                last.then_inc(t_mm.sem, 1)
                pe.wait_ge(t_in.sem, t_in.at(3))
                for t in range(NPAIR):
                    last = nc.tensor.transpose(ps[0][:, t * P:(t + 1) * P], att[:, t, :], ident[:])
                last.then_inc(t_tr.sem, 1)
                pe.wait_ge(t_cp.sem, t_cp.at(4))
                for t in range(NPAIR):
                    last = nc.tensor.matmul(ps[2 + t // 2][:, (t % 2) * F:(t % 2) * F + F], attT[:, t, :], vo[:, t, :],
                                            start=True, stop=True)
                last.then_inc(t_mm.sem, 1)
        for t, k in ((t_in, 3), (t_tr, 3), (t_cp, 4), (t_mm, 5), (m_mm, 1), (m_out, 2 * NPAIR)):
            t.close(k)

        with nc.Block() as block:
            @block.scalar
            def _(act):
                with act.Fori(0, NC // U) as i:
                    for j in range(U):
                        n = i * U + j
                        act.wait_ge(t_mm.sem, t_mm.at(n + early(j)))
                        nc.scalar.copy(wn[:, j % 2, :], WT[:, bass.ds(n, 1), :].rearrange("p a k -> p (a k)")
                                       ).then_inc(t_in.sem, 1)

            @block.tensor
            def _(pe):
                with pe.Fori(0, NC // U) as i:
                    for j in range(U):
                        n = i * U + j
                        pe.wait_ge(t_in.sem, t_in.at(n + 1))
                        pe.wait_ge(t_out.sem, t_out.at(n + early(j)))
                        for t in range(NPAIR):
                            last = nc.tensor.matmul(ps[j % 2][:, 0:F], wn[:, j % 2, t * P:(t + 1) * P], om[:, t, :],
                                                    start=(t == 0), stop=(t == NPAIR - 1))
                        last.then_inc(t_mm.sem, 1)

            @block.vector
            def _(dve):
                step = Chain(dve, ch)
                with dve.Fori(0, NC // U) as i:
                    step.enter(i, U * 2)
                    for j in range(U):
                        n = i * U + j
                        dve.wait_ge(t_mm.sem, t_mm.at(n + 1))
                        step(nc.vector.tensor_tensor(wk[:, j % 2, 0:F], ps[j % 2][:, 0:F], bias[:, 1, :], ALU.add))
                        dve.sem_inc(t_out.sem, 1)
                        step(nc.vector.tensor_tensor(row(XR, n), row(XR, n), wk[:, j % 2, 0:F], ALU.add))
                step.leave(NC // U)
                ch.close(step.done)
        for t in (t_in, t_mm, t_out):
            t.close(NC)

        def scale_rows(k):
            def prepare(dve, step, c, dst_tile):
                step(nc.vector.tensor_scalar(dst_tile, row(R, c), invs[:, k, bass.ds(c, 1)], None, ALU.mult))
            return prepare

        normalise()
        sum_over_edges(0, 1, at_dram, from_z(None))
        sum_over_edges(1, 0, a_dram, mean_of_sums)

        def prelu(step, to, t):
            step(nc.vector.tensor_scalar(wk[:, 1, 0:F], t, 0.0, slope[:, 0:1], ALU.min, ALU.mult))
            step(nc.vector.scalar_tensor_tensor(to, t, 0.0, wk[:, 1, 0:F], ALU.max, ALU.add))

        def put_h(dve, step, c, prod):
            step(nc.vector.tensor_tensor(wk[:, 0, 0:F], prod, bias[:, 2, :], ALU.add))
            prelu(step, row(S, c), wk[:, 0, 0:F])
            step(nc.vector.tensor_reduce(hmax[:, bass.ds(c, 1)], row(S, c), AX.X, ALU.max, apply_absolute_value=True))

        graph_product(1, scale_rows(0), 1, put_h, 4)
        with nc.Block() as block:
            @block.vector
            def _(dve):
                step = Chain(dve, ch)
                step(nc.vector.tensor_reduce(hmax[:, NC:NC + 1], hmax[:, 0:NC], AX.X, ALU.max))
                dve.sem_inc(t_in.sem, 1)
                dve.wait_ge(t_tr.sem, t_tr.at(1))
                step(nc.vector.tensor_reduce(hmax[0:1, NC + 1:NC + 2], ps[0][0:1, 0:P], AX.X, ALU.max))
                dve.sem_inc(t_in.sem, 1)
                dve.wait_ge(t_mm.sem, t_mm.at(1))
                step(nc.vector.tensor_scalar(hmax[:, NC:NC + 1], ps[1][:, 0:1], 1e-30, 1.0 / BIGH, ALU.max, ALU.mult))
                nc.vector.tensor_scalar(invs[:, 1, :], inv[:, 0, :], hmax[:, NC:NC + 1], None, ALU.mult)
                step(nc.vector.reciprocal(hmax[:, NC + 2:NC + 3], hmax[:, NC:NC + 1]))
                ch.close(step.done)

            @block.tensor
            def _(pe):
                pe.wait_ge(t_in.sem, t_in.at(1))
                nc.tensor.transpose(ps[0][0:1, 0:P], hmax[:, NC:NC + 1], ident[:]).then_inc(t_tr.sem, 1)
                pe.wait_ge(t_in.sem, t_in.at(2))
                nc.tensor.matmul(ps[1][:, 0:1], ones[0:1, :], hmax[0:1, NC + 1:NC + 2], start=True, stop=True
                                 ).then_inc(t_mm.sem, 1)
        t_in.close(2)
        t_tr.close(1)
        t_mm.close(1)
        sum_over_edges(0, 1, at_dram, scaled_h)
        sum_over_edges(1, 0, a_dram, mean_of_sums)

        def put_l1(dve, step, c, prod):
            step(nc.vector.tensor_tensor(wk[:, 0, 0:F], prod, bias[:, 3, :], ALU.add))
            step(nc.vector.tensor_tensor(wk[:, 0, 0:F], wk[:, 0, 0:F], row(Z, c), ALU.add))
            prelu(step, wk[:, 0, F:2 * F], wk[:, 0, 0:F])
            step(nc.vector.tensor_tensor(row(XR, c), row(XR, c), wk[:, 0, F:2 * F], ALU.add))

        graph_product(2, scale_rows(1), 1, put_l1, 5)
        normalise()

        w1 = BIG[:, 0:KF * X * HID].rearrange("p (k e n) -> p k e n", k=KF, e=X)
        w2 = BIG[:, KF * X * HID:2 * KF * X * HID].rearrange("p (k e n) -> p k e n", k=KH, e=X)
        b1 = XB[:, 0:X * HID].rearrange("p (e n) -> p e n", e=X)
        b2 = XB[:, X * HID:X * (HID + F)].rearrange("p (e n) -> p e n", e=X)
        gwt = gw[:, 0, :, 0:X]
        gbb = gw[:, 1, 0, 0:X]
        def table(m, w=NC * X):
            return SR[:, m * NC * X:m * NC * X + w]
        lg, prob, one1, one2, tmp, pick, rank, slot = (
            table(m).rearrange("p (c e) -> p c e", e=X) for m in range(8))
        tot = table(8)
        cum = table(9)
        mx, mx2, sx = table(10, NC), table(11, NC), table(12, NC)
        slots_f = table(13, 2 * NC).rearrange("p (k c) -> p k c", k=2)
        slots_i = table(14, 2 * NC).bitcast(I32).rearrange("p (k c) -> p k c", k=2)
        gk = table(15, 2 * NC).rearrange("p (k c) -> p k c", k=2)
        keep = table(16)
        ie = table(17, X)
        cnt = table(18, X)
        basee = table(19, X)
        tile_e = table(20, TILES)
        tile_i = table(21, TILES).bitcast(I32)
        tix = table(22, TILES)
        cmp = SR[:, 23 * NC * X:23 * NC * X + TILES * X].rearrange("p (t e) -> p t e", e=X)
        oc = SR[:, 6400:6400 + 12 * 2 * F]
        with nc.Block() as block:
            @block.sync
            def _(sp):
                for k in range(KF):
                    sp.dma_start(w1[:, k], e_w1.rearrange("e (k p) n -> k p e n", p=P)[k]).then_inc(ld.sem, 16)
                for k in range(KH):
                    sp.dma_start(w2[:, k], e_w2.rearrange("e (k p) n -> k p e n", p=P)[k]).then_inc(ld.sem, 16)
                sp.dma_start(gwt, gate_w.rearrange("(k p) e -> p k e", p=P)).then_inc(ld2.sem, 16)
                sp.dma_start(gbb, gate_b.partition_broadcast(P)).then_inc(ld2.sem, 16)
                for t in range(TILES):
                    sp.dma_start(xs_dram[t * P:(t + 1) * P, :], zeros[:, 0:F]).then_inc(st.sem, 16)
                sp.wait_ge(st.sem, st.at(16 * TILES))
                sp.wait_ge(ld.sem, ld.at(16 * (KF + KH)))
                sp.wait_ge(ld2.sem, ld2.at(32))

            @block.gpsimd
            def _(pool):
                pool.iota(ie, [[1, X]], base=0, channel_multiplier=0, allow_small_or_imprecise_dtypes=True)
                pool.iota(tix, [[P, TILES]], base=0, channel_multiplier=0, allow_small_or_imprecise_dtypes=True)
        st.close(16 * TILES)
        ld.close(16 * (KF + KH))
        ld2.close(32)
        with nc.Block() as block:
            @block.vector
            def _(dve):
                step = Chain(dve, ch)
                with dve.Fori(0, NC // U) as i:
                    step.enter(i, U)
                    for j in range(U):
                        n = i * U + j
                        dve.wait_ge(t_tr.sem, t_tr.at(n + early(j)))
                        nc.vector.tensor_copy(tb[:, j % 2, :], row(Z, n)).then_inc(t_in.sem, 1)
                        dve.wait_ge(t_mm.sem, t_mm.at(n + 1))
                        step(nc.vector.tensor_tensor(lg[:, bass.ds(n, 1), :].rearrange("p a e -> p (a e)"),
                                                     ps[2 + j % 2][:, 0:X], gbb, ALU.add))
                        dve.sem_inc(t_out.sem, 1)
                step.leave(NC // U)
                ch.close(step.done)

            @block.scalar
            def _(act):
                with act.Fori(0, NC // U) as i:
                    for j in range(U):
                        n = i * U + j
                        act.wait_ge(t_tr.sem, t_tr.at(n + 1))
                        act.wait_ge(t_mm.sem, t_mm.at(n + early(j)))
                        nc.scalar.copy(tT[:, j % 2, :], ps[j % 2][:, 0:F]).then_inc(t_cp.sem, 1)

            @block.tensor
            def _(pe):
                with pe.Fori(0, NC // U) as i:
                    for j in range(U):
                        n = i * U + j
                        pe.wait_ge(t_in.sem, t_in.at(n + 1))
                        pe.wait_ge(t_cp.sem, t_cp.at(n + early(j)))
                        for k in range(KF):
                            last = nc.tensor.transpose(ps[j % 2][:, k * P:(k + 1) * P],
                                                       tb[:, j % 2, k * P:(k + 1) * P], ident[:])
                        last.then_inc(t_tr.sem, 1)
                        pe.wait_ge(t_cp.sem, t_cp.at(n + 1))
                        pe.wait_ge(t_out.sem, t_out.at(n + early(j)))
                        for k in range(KF):
                            last = nc.tensor.matmul(ps[2 + j % 2][:, 0:X], tT[:, j % 2, k * P:(k + 1) * P],
                                                    gwt[:, k, :], start=(k == 0), stop=(k == KF - 1))
                        last.then_inc(t_mm.sem, 1)
        for t in (t_in, t_tr, t_cp, t_mm, t_out):
            t.close(NC)

        def over(t2):
            return t2.unsqueeze(2).to_broadcast([P, NC, X])

        ie3 = ie.unsqueeze(1).to_broadcast([P, NC, X])
        with nc.Block() as block:
            @block.vector
            def _(dve):
                step = Chain(dve, ch)
                step(nc.vector.tensor_reduce(mx, lg, AX.X, ALU.max))
                step(nc.vector.tensor_tensor(lg, lg, over(mx), ALU.subtract))
                dve.sem_inc(t_in.sem, 1)
                dve.wait_ge(t_cp.sem, t_cp.at(1))
                step(nc.vector.tensor_reduce(sx, prob, AX.X, ALU.add))
                step(nc.vector.reciprocal(sx, sx))
                step(nc.vector.tensor_tensor(prob, prob, over(sx), ALU.mult))
                step(nc.vector.tensor_copy(keep.rearrange("p (c e) -> p c e", e=X), prob))
                left = keep.rearrange("p (c e) -> p c e", e=X)
                for k, one in enumerate((one1, one2)):
                    top = gk[:, k, :]
                    step(nc.vector.tensor_reduce(top, left, AX.X, ALU.max))
                    step(nc.vector.tensor_tensor(tmp, left, over(top), ALU.is_lt))
                    step(nc.vector.scalar_tensor_tensor(tmp, tmp, float(X), ie3, ALU.mult, ALU.add))
                    step(nc.vector.tensor_reduce(mx2, tmp, AX.X, ALU.min))
                    step(nc.vector.tensor_tensor(one, ie3, over(mx2), ALU.is_equal))
                    step(nc.vector.scalar_tensor_tensor(left, one, -2.0, left, ALU.mult, ALU.add))
                step(nc.vector.tensor_tensor(pick, one1, one2, ALU.add))
                step(nc.vector.tensor_tensor(pick, pick, over(valid[:]), ALU.mult))
                dve.sem_inc(t_in.sem, 1)
                dve.wait_ge(t_mm.sem, t_mm.at(1))
                nc.vector.tensor_copy(rank.rearrange("p c e -> p (c e)"), ps[0][:, 0:NC * X])
                step(nc.vector.tensor_copy(tot.rearrange("p (e c) -> p e c", e=X),
                                           ps[1][:, 0:NC * X].rearrange("p (c e) -> p e c", e=X)))
                for e in range(X):
                    at = slice(e * NC, (e + 1) * NC)
                    last = nc.vector.tensor_tensor_scan(cum[:, at], tot[:, at], tot[:, at], 0.0, ALU.add, ALU.bypass)
                step(last)
                step(nc.vector.tensor_copy(cnt, cum.rearrange("p (e c) -> p e c", e=X)[:, :, NC - 1]))
                step(nc.vector.tensor_tensor(cum, cum, tot, ALU.subtract))
                step(nc.vector.tensor_tensor(cmp, tix.unsqueeze(2).to_broadcast([P, TILES, X]),
                                             cnt.unsqueeze(1).to_broadcast([P, TILES, X]), ALU.is_lt))
                step(nc.vector.tensor_reduce(cnt, cmp.rearrange("p t e -> p e t"), AX.X, ALU.add))
                step(nc.vector.tensor_tensor_scan(basee, cnt, cnt, 0.0, ALU.add, ALU.bypass))
                step(nc.vector.tensor_scalar(tmp[:, 0, :], basee, float(P), None, ALU.mult))
                step(nc.vector.tensor_tensor(cmp, tix.unsqueeze(2).to_broadcast([P, TILES, X]),
                                             tmp[:, 0, :].unsqueeze(1).to_broadcast([P, TILES, X]), ALU.is_ge))
                step(nc.vector.tensor_reduce(tile_e, cmp, AX.X, ALU.add))
                step(nc.vector.tensor_scalar(tile_e, tile_e, float(X - 1), None, ALU.min))
                step(nc.vector.tensor_copy(tile_i, tile_e))
                step(nc.vector.tensor_tensor(basee, basee, cnt, ALU.subtract))
                step(nc.vector.tensor_scalar(basee, basee, float(P), None, ALU.mult))
                step(nc.vector.tensor_tensor(slot, rank, cum.rearrange("p (e c) -> p c e", e=X), ALU.add))
                step(nc.vector.tensor_tensor(slot, slot, basee.unsqueeze(1).to_broadcast([P, NC, X]), ALU.add))
                for k, one in enumerate((one1, one2)):
                    step(nc.vector.tensor_tensor(tmp, slot, one, ALU.mult))
                    step(nc.vector.tensor_reduce(slots_f[:, k, :], tmp, AX.X, ALU.add))
                step(nc.vector.tensor_scalar(mx, valid[:], -float(4 * SLOTS), float(4 * SLOTS), ALU.mult, ALU.add))
                for k in range(2):
                    step(nc.vector.tensor_tensor(slots_f[:, k, :], slots_f[:, k, :], mx, ALU.add))
                step(nc.vector.tensor_copy(slots_i, slots_f))
                ch.close(step.done)

            @block.scalar
            def _(act):
                act.wait_ge(t_in.sem, t_in.at(1))
                nc.scalar.activation(prob, lg, ACT.Exp).then_inc(t_cp.sem, 1)

            @block.tensor
            def _(pe):
                pe.wait_ge(t_in.sem, t_in.at(2))
                nc.tensor.matmul(ps[0][:, 0:NC * X], before[:], pick.rearrange("p c e -> p (c e)"), start=True, stop=True)
                nc.tensor.matmul(ps[1][:, 0:NC * X], ones[:], pick.rearrange("p c e -> p (c e)"), start=True, stop=True
                                 ).then_inc(t_mm.sem, 1)
        for t, k in ((t_in, 2), (t_cp, 1), (t_mm, 1)):
            t.close(k)

        with nc.Block() as block:
            @block.gpsimd
            def _(pool):
                for c in range(NC):
                    for k in range(2):
                        pool.indirect_dma_start(
                            out=xs_dram, in_=Z[:, c, 0:F], in_offset=None,
                            out_offset=bass.IndirectOffsetOnAxis(ap=slots_i[:, k, c:c + 1], axis=0),
                            bounds_check=SLOTS - 1, oob_is_err=False).then_inc(ysem[k].sem, 16)
                for k in range(2):
                    pool.wait_ge(ysem[k].sem, ysem[k].at(16 * NC))
        for t in ysem:
            t.close(16 * NC)
        with nc.Block() as block:
            @block.sync
            def _(sp):
                sp.dma_start(b1.rearrange("p e n -> p (e n)"), e_b1.rearrange("e n -> (e n)").partition_broadcast(P)).then_inc(ld.sem, 16)
                sp.dma_start(b2.rearrange("p e n -> p (e n)"), e_b2.rearrange("e n -> (e n)").partition_broadcast(P)).then_inc(ld.sem, 16)
                sp.wait_ge(ld.sem, ld.at(32))
        ld.close(32)

        UT = 2
        assert TILES % UT == 0
        hT = wk
        with nc.Block() as block:
            @block.sync
            def _(sp):
                with sp.Fori(0, TILES // UT) as i:
                    for j in range(UT):
                        n = i * UT + j
                        if j == 0:
                            sp.wait_ge(t_tr.sem, t_tr.at(n))
                        else:
                            sp.wait_ge(t_tr.sem, t_tr.at(n - 1))
                        sp.dma_start(tb[:, j, :], xs_dram[bass.ds(n * P, P), :]).then_inc((ld, ld2)[j].sem, 16)

            @block.tensor
            def _(pe):
                with pe.Fori(0, TILES // UT) as i:
                    for j in range(UT):
                        n = i * UT + j
                        pe.wait_ge((ld, ld2)[j].sem, (ld, ld2)[j].at(16 * i + 16))
                        pe.wait_ge(m_cp.sem, m_cp.at(n - j))
                        expert = pe.value_load(tile_i[0:1, bass.ds(n, 1)], min_val=0, max_val=X - 1)
                        for k in range(KF):
                            last = nc.tensor.transpose(ps[j][:, k * P:(k + 1) * P], tb[:, j, k * P:(k + 1) * P], ident[:])
                        last.then_inc(t_tr.sem, 1)
                        pe.wait_ge(t_cp.sem, t_cp.at(n + 1))
                        pe.wait_ge(t_out.sem, t_out.at(n - j))
                        for k in range(KF):
                            last = nc.tensor.matmul(ps[2 + j][:, :], tT[:, j, k * P:(k + 1) * P],
                                                    w1[:, k, bass.ds(expert, 1), :].rearrange("p a n -> p (a n)"),
                                                    start=(k == 0), stop=(k == KF - 1))
                        last.then_inc(t_mm.sem, 1)
                        pe.wait_ge(m_mm.sem, m_mm.at(n + 1))
                        for k in range(KH):
                            last = nc.tensor.transpose(ps[j][:, k * P:(k + 1) * P], wn[:, j, k * P:(k + 1) * P], ident[:])
                        last.then_inc(m_tr.sem, 1)
                        pe.wait_ge(m_cp.sem, m_cp.at(n + 1))
                        pe.wait_ge(n_b.sem, n_b.at(n - j))
                        for k in range(KH):
                            last = nc.tensor.matmul(ps[4 + j][:, 0:F], hT[:, j, k * P:(k + 1) * P],
                                                    w2[:, k, bass.ds(expert, 1), :].rearrange("p a n -> p (a n)"),
                                                    start=(k == 0), stop=(k == KH - 1))
                        last.then_inc(n_a.sem, 1)

            @block.vector
            def _(dve):
                with dve.Fori(0, TILES // UT) as i:
                    for j in range(UT):
                        n = i * UT + j
                        expert = dve.value_load(tile_i[0:1, bass.ds(n, 1)], min_val=0, max_val=X - 1)
                        dve.wait_ge(t_mm.sem, t_mm.at(n + 1))
                        dve.wait_ge(m_tr.sem, m_tr.at(n - j))
                        nc.vector.tensor_tensor(wn[:, j, :], ps[2 + j][:, :],
                                                b1[:, bass.ds(expert, 1), :].rearrange("p a n -> p (a n)"), ALU.add
                                                ).then_inc(t_out.sem, 1)
                        dve.wait_ge(m_tr.sem, m_tr.at(n + 1))
                        dve.wait_ge(n_a.sem, n_a.at(n - j))
                        nc.vector.tensor_copy(hT[:, j, :], ps[j][:, :]).then_inc(m_cp.sem, 1)
                        dve.wait_ge(n_a.sem, n_a.at(n + 1))
                        dve.wait_ge(ysem[j].sem, ysem[j].at(16 * i))
                        nc.vector.tensor_tensor(sm2[:, j, :], ps[4 + j][:, 0:F],
                                                b2[:, bass.ds(expert, 1), :].rearrange("p a n -> p (a n)"), ALU.add
                                                ).then_inc(n_b.sem, 1)

            @block.scalar
            def _(act):
                with act.Fori(0, TILES // UT) as i:
                    for j in range(UT):
                        n = i * UT + j
                        act.wait_ge(t_tr.sem, t_tr.at(n + 1))
                        act.wait_ge(t_mm.sem, t_mm.at(n - j))
                        nc.scalar.copy(tT[:, j, :], ps[j][:, 0:F]).then_inc(t_cp.sem, 1)
                        act.wait_ge(t_out.sem, t_out.at(n + 1))
                        nc.scalar.activation(wn[:, j, :], wn[:, j, :], ACT.Gelu).then_inc(m_mm.sem, 1)

            @block.gpsimd
            def _(pool):
                with pool.Fori(0, TILES // UT) as i:
                    for j in range(UT):
                        n = i * UT + j
                        pool.wait_ge(n_b.sem, n_b.at(n + 1))
                        pool.dma_start(ys_dram[bass.ds(n * P, P), :], sm2[:, j, :]).then_inc(ysem[j].sem, 16)
                for j in range(UT):
                    pool.wait_ge(ysem[j].sem, ysem[j].at(16 * (TILES // UT)))
        for t in (t_tr, t_cp, t_mm, t_out, m_mm, m_tr, m_cp, n_a, n_b):
            t.close(TILES)
        for t in (*ysem, ld, ld2):
            t.close(16 * (TILES // UT))

        oc4 = oc.rearrange("p (b k f) -> p b k f", k=2, f=F)
        NB = 12
        with nc.Block() as block:
            @block.gpsimd
            def _(pool):
                pool.memset(oc, 0.0).then_inc(chp.sem, 1)
                pool.wait_ge(chp.sem, chp.at(1))
                for c in range(NC):
                    if c >= NB:
                        pool.wait_ge(t_out.sem, t_out.at(c - NB + 1))
                    for k in range(2):
                        pool.indirect_dma_start(
                            out=oc4[:, c % NB, k, :], out_offset=None, in_=ys_dram,
                            in_offset=bass.IndirectOffsetOnAxis(ap=slots_i[:, k, c:c + 1], axis=0),
                            bounds_check=SLOTS - 1, oob_is_err=False).then_inc(gs[c % NB].sem, 16)

            @block.vector
            def _(dve):
                step = Chain(dve, ch)
                for c in range(NC):
                    dve.wait_ge(gs[c % NB].sem, 32 * (c // NB + 1))
                    step(nc.vector.scalar_tensor_tensor(XR[:, c, :], oc4[:, c % NB, 0, :], gk[:, 0, c:c + 1],
                                                        XR[:, c, :], ALU.mult, ALU.add))
                    step(nc.vector.scalar_tensor_tensor(XR[:, c, :], oc4[:, c % NB, 1, :], gk[:, 1, c:c + 1],
                                                        XR[:, c, :], ALU.mult, ALU.add))
                    dve.sem_inc(t_out.sem, 1)
                ch.close(step.done)

            @block.sync
            def _(sp):
                sp.wait_ge(t_out.sem, t_out.at(NC))
                sp.dma_start(out[0:(NC - 1) * P, :].rearrange("(c p) f -> p c f", p=P), XR[:, 0:NC - 1, :]).then_inc(st.sem, 16)
                sp.dma_start(out[(NC - 1) * P:N, :], XR[0:LAST, NC - 1, :]).then_inc(st.sem, 16)
                sp.wait_ge(st.sem, st.at(32))


_INS = ['x', 'src', 'dst', 'L0_gnn_W', 'L0_gnn_b', 'L0_ffn_W_fx', 'L0_ffn_b_fx', 'L0_ffn_W_x', 'L0_ffn_b_x',
        'L0_ffn_W_slice', 'L0_ffn_b_slice', 'L0_ffn_W_q', 'L0_ffn_W_k', 'L0_ffn_W_v', 'L0_ffn_W_out',
        'L0_ffn_b_out', 'L0_ffn_temperature', 'L1_gnn_W1', 'L1_gnn_b1', 'L1_gnn_W2', 'L1_gnn_b2', 'L1_gnn_a',
        'L1_ffn_gate_w', 'L1_ffn_gate_b', 'L1_ffn_W1', 'L1_ffn_b1', 'L1_ffn_W2', 'L1_ffn_b2']


def kernel(**inputs):
    import concourse.bacc as bacc
    from concourse.bass_utils import run_bass_kernel_spmd

    nc = bacc.Bacc("TRN2", target_bir_lowering=False, num_devices=1)
    arrays, args = {}, []
    for name in _INS:
        a = np.ascontiguousarray(inputs[name])
        arrays[f"in_{name}"] = a
        args.append(nc.dram_tensor(f"in_{name}", a.shape, mybir.dt.from_np(a.dtype), kind="ExternalInput").ap())
    args.append(nc.dram_tensor("out_0", (N, F), F32, kind="ExternalOutput").ap())
    build(nc, *args)
    r = run_bass_kernel_spmd(nc, [arrays], core_ids=[0])
    return r.results[0]["out_0"]
```
